# Optimizing a Trainium2 kernel written in Bass

```python
import numpy as np
import jax
import jax.numpy as jnp

def _softmax(x, axis=-1):
    return jax.nn.softmax(x, axis=axis)

def _gelu(x):
    return jax.nn.gelu(x, approximate=True)

def _silu(x):
    return jax.nn.silu(x)

def _sigmoid(x):
    return jax.nn.sigmoid(x)

def _layernorm(x, axis=-1, eps=1e-05):
    m = jnp.mean(x, axis=axis, keepdims=True)
    v = jnp.var(x, axis=axis, keepdims=True)
    return (x - m) / jnp.sqrt(v + eps)

def _scatter_add(tgt, idx, src, axis=0):
    return tgt.at[idx].add(src)

def _segment_sum(src, seg, n):
    return jax.ops.segment_sum(src, seg, n)
kernel_name = 'mk_sandwich_d1_jaxref_r8_802bb1'

def setup_inputs(seed: int=0):
    np.random.seed(seed)
    _w = jnp.asarray

    def _L0_attn_setup():
        import jax, jax.numpy as jnp
        import numpy as np
        from jax import lax
        D_MODEL, D_STATE, D_CONV, EXPAND = (128, 16, 4, 2)
        D_INNER = EXPAND * D_MODEL
        DT_RANK = (D_MODEL + 15) // 16
        B, T = (4, 256)

        def _causal_depthwise_conv(xb, conv_w, conv_b):
            inp = xb.transpose(0, 2, 1)
            ker = conv_w[:, None, :]
            dn = lax.conv_dimension_numbers(inp.shape, ker.shape, ('NCH', 'OIH', 'NCH'))
            out = lax.conv_general_dilated(inp, ker, window_strides=(1,), padding=[(D_CONV - 1, 0)], dimension_numbers=dn, feature_group_count=D_INNER)
            return (out + conv_b[None, :, None]).transpose(0, 2, 1)
        key = jax.random.key(seed)
        ks = jax.random.split(key, 10)
        s = lambda fan_in: 1.0 / np.sqrt(fan_in)
        return {'x': jax.random.normal(ks[0], (B, T, D_MODEL), dtype=jnp.float32), 'in_proj_w': jax.random.normal(ks[1], (D_MODEL, 2 * D_INNER), dtype=jnp.float32) * s(D_MODEL), 'conv_w': jax.random.normal(ks[2], (D_INNER, D_CONV), dtype=jnp.float32) * s(D_CONV), 'conv_b': jax.random.normal(ks[3], (D_INNER,), dtype=jnp.float32) * 0.1, 'x_proj_w': jax.random.normal(ks[4], (D_INNER, DT_RANK + 2 * D_STATE), dtype=jnp.float32) * s(D_INNER), 'dt_proj_w': jax.random.normal(ks[5], (DT_RANK, D_INNER), dtype=jnp.float32) * s(DT_RANK), 'dt_proj_b': jax.random.normal(ks[6], (D_INNER,), dtype=jnp.float32) * 0.1, 'A_log': jax.random.normal(ks[7], (D_INNER, D_STATE), dtype=jnp.float32) * 0.5, 'D_param': jnp.ones((D_INNER,), dtype=jnp.float32), 'out_proj_w': jax.random.normal(ks[8], (D_INNER, D_MODEL), dtype=jnp.float32) * s(D_INNER)}
    _L0_attn_in = _L0_attn_setup()

    def _L0_ffn_setup():
        import jax, jax.numpy as jnp
        import numpy as np
        DIM = 128
        DEPTH = 2
        HEADS = 8
        DIM_HEAD = 64
        WINDOW = 64
        INNER = HEADS * DIM_HEAD
        HID = int(DIM * 4 * 2 / 3)
        B, N = (2, 1024)
        QK_SCALE = 8.0

        def shift_token(t):
            t1, t2 = jnp.split(t, 2, axis=-1)
            t2 = jnp.pad(t2, ((0, 0), (1, 0), (0, 0)))[:, :-1]
            return jnp.concatenate([t1, t2], axis=-1)

        def l2norm(t):
            return t / jnp.clip(jnp.linalg.norm(t, axis=-1, keepdims=True), 1e-12)

        def rotate_half(x):
            x1, x2 = jnp.split(x, 2, axis=-1)
            return jnp.concatenate([-x2, x1], axis=-1)

        def rotary_xpos(q, k):
            n = q.shape[-2]
            half_idx = jnp.arange(0, DIM_HEAD, 2, dtype=jnp.float32)
            inv_freq = 1.0 / 10000.0 ** (half_idx / DIM_HEAD)
            t = jnp.arange(n, dtype=jnp.float32)
            freqs = t[:, None] * inv_freq[None, :]
            freqs = jnp.concatenate([freqs, freqs], axis=-1)
            base = (half_idx + 0.4 * DIM_HEAD) / (1.4 * DIM_HEAD)
            power = (t - n // 2) / float(WINDOW // 2)
            scale = base[None, :] ** power[:, None]
            scale = jnp.concatenate([scale, scale], axis=-1)
            cos, sin = (jnp.cos(freqs), jnp.sin(freqs))
            q = q * cos * scale + rotate_half(q) * sin * scale
            k = k * cos / scale + rotate_half(k) * sin / scale
            return (q, k)

        def local_attention(q, k, v):
            b, h, n, d = q.shape
            w = n // WINDOW
            bq = q.reshape(b, h, w, WINDOW, d) * QK_SCALE
            bk = k.reshape(b, h, w, WINDOW, d)
            bv = v.reshape(b, h, w, WINDOW, d)

            def look_around(t):
                p = jnp.pad(t, ((0, 0), (0, 0), (1, 0), (0, 0), (0, 0)))
                return jnp.concatenate([p[:, :, :w], p[:, :, 1:]], axis=3)
            bk, bv = (look_around(bk), look_around(bv))
            bt = jnp.arange(n).reshape(w, WINDOW)
            btp = jnp.pad(bt, ((1, 0), (0, 0)), constant_values=-1)
            btk = jnp.concatenate([btp[:w], btp[1:]], axis=1)
            sim = jnp.einsum('bhwid,bhwjd->bhwij', bq, bk)
            i = bt[:, :, None]
            j = btk[:, None, :]
            mask = (i < j) | (i > j + WINDOW) | (j == -1)
            sim = jnp.where(mask, -jnp.finfo(sim.dtype).max, sim)
            attn = jax.nn.softmax(sim, axis=-1)
            out = jnp.einsum('bhwij,bhwjd->bhwid', attn, bv)
            return out.reshape(b, h, n, d)

        def _layer(x, wqkv, qs, ksc, wo, lg, lb, w1, b1, w2, b2):
            b, n, _ = x.shape
            h = shift_token(x)
            qkv = h @ wqkv
            q, k, v = jnp.split(qkv, 3, axis=-1)
            to_heads = lambda t: t.reshape(b, n, HEADS, DIM_HEAD).transpose(0, 2, 1, 3)
            q, k, v = (to_heads(q), to_heads(k), to_heads(v))
            q = l2norm(q) * qs
            k = l2norm(k) * ksc
            q, k = rotary_xpos(q, k)
            o = local_attention(q, k, v)
            o = o.transpose(0, 2, 1, 3).reshape(b, n, INNER)
            x = x + o @ wo
            h = shift_token(x)
            mu = h.mean(-1, keepdims=True)
            var = h.var(-1, keepdims=True)
            h = (h - mu) / jnp.sqrt(var + 1e-05) * lg + lb
            h = h @ w1 + b1
            a, g = jnp.split(h, 2, axis=-1)
            h = a * jax.nn.gelu(g, approximate=False)
            x = x + h @ w2 + b2
            return x
        key = jax.random.key(seed)
        ks = jax.random.split(key, 6)
        return {'x': jax.random.normal(ks[0], (B, N, DIM), jnp.float32), 'wqkv': jax.random.normal(ks[1], (DEPTH, DIM, 3 * INNER), jnp.float32) * 0.02, 'q_scale': jnp.ones((DEPTH, DIM_HEAD), jnp.float32), 'k_scale': jnp.ones((DEPTH, DIM_HEAD), jnp.float32), 'wo': jax.random.normal(ks[2], (DEPTH, INNER, DIM), jnp.float32) * 0.02, 'ln_g': jnp.ones((DEPTH, DIM), jnp.float32), 'ln_b': jnp.zeros((DEPTH, DIM), jnp.float32), 'w1': jax.random.normal(ks[3], (DEPTH, DIM, 2 * HID), jnp.float32) * 0.02, 'b1': jnp.zeros((DEPTH, 2 * HID), jnp.float32), 'w2': jax.random.normal(ks[4], (DEPTH, HID, DIM), jnp.float32) * 0.02, 'b2': jnp.zeros((DEPTH, DIM), jnp.float32)}
    _L0_ffn_in = _L0_ffn_setup()
    _d = {'L0_attn_x': _L0_attn_in['x'], 'L0_attn_in_proj_w': _L0_attn_in['in_proj_w'], 'L0_attn_conv_w': _L0_attn_in['conv_w'], 'L0_attn_conv_b': _L0_attn_in['conv_b'], 'L0_attn_x_proj_w': _L0_attn_in['x_proj_w'], 'L0_attn_dt_proj_w': _L0_attn_in['dt_proj_w'], 'L0_attn_dt_proj_b': _L0_attn_in['dt_proj_b'], 'L0_attn_A_log': _L0_attn_in['A_log'], 'L0_attn_D_param': _L0_attn_in['D_param'], 'L0_attn_out_proj_w': _L0_attn_in['out_proj_w'], 'L0_ffn_wqkv': _L0_ffn_in['wqkv'], 'L0_ffn_q_scale': _L0_ffn_in['q_scale'], 'L0_ffn_k_scale': _L0_ffn_in['k_scale'], 'L0_ffn_wo': _L0_ffn_in['wo'], 'L0_ffn_ln_g': _L0_ffn_in['ln_g'], 'L0_ffn_ln_b': _L0_ffn_in['ln_b'], 'L0_ffn_w1': _L0_ffn_in['w1'], 'L0_ffn_b1': _L0_ffn_in['b1'], 'L0_ffn_w2': _L0_ffn_in['w2'], 'L0_ffn_b2': _L0_ffn_in['b2']}
    _x0 = _d['L0_attn_x']
    _d['L0_attn_x'] = jax.random.normal(jax.random.fold_in(jax.random.key(seed), 1), (16, 512, 128), dtype=_x0.dtype)
    del _x0
    return _d

def reference(L0_attn_x, L0_attn_in_proj_w, L0_attn_conv_w, L0_attn_conv_b, L0_attn_x_proj_w, L0_attn_dt_proj_w, L0_attn_dt_proj_b, L0_attn_A_log, L0_attn_D_param, L0_attn_out_proj_w, L0_ffn_wqkv, L0_ffn_q_scale, L0_ffn_k_scale, L0_ffn_wo, L0_ffn_ln_g, L0_ffn_ln_b, L0_ffn_w1, L0_ffn_b1, L0_ffn_w2, L0_ffn_b2):

    def _L0_attn_ref(x, in_proj_w, conv_w, conv_b, x_proj_w, dt_proj_w, dt_proj_b, A_log, D_param, out_proj_w):
        import jax, jax.numpy as jnp
        import numpy as np
        from jax import lax
        D_MODEL, D_STATE, D_CONV, EXPAND = (128, 16, 4, 2)
        D_INNER = EXPAND * D_MODEL
        DT_RANK = (D_MODEL + 15) // 16
        B, T = (4, 256)

        def _causal_depthwise_conv(xb, conv_w, conv_b):
            inp = xb.transpose(0, 2, 1)
            ker = conv_w[:, None, :]
            dn = lax.conv_dimension_numbers(inp.shape, ker.shape, ('NCH', 'OIH', 'NCH'))
            out = lax.conv_general_dilated(inp, ker, window_strides=(1,), padding=[(D_CONV - 1, 0)], dimension_numbers=dn, feature_group_count=D_INNER)
            return (out + conv_b[None, :, None]).transpose(0, 2, 1)
        xz = x @ in_proj_w
        xb, z = jnp.split(xz, 2, axis=-1)
        xb = jax.nn.silu(_causal_depthwise_conv(xb, conv_w, conv_b))
        proj = xb @ x_proj_w
        dt = jax.nn.softplus(proj[..., :DT_RANK] @ dt_proj_w + dt_proj_b)
        b = proj[..., DT_RANK:DT_RANK + D_STATE]
        c = proj[..., DT_RANK + D_STATE:]
        a = -jnp.exp(A_log)

        def step(state, ts):
            u_t, dt_t, b_t, c_t = ts
            da = jnp.exp(dt_t[:, :, None] * a)
            dbu = dt_t[:, :, None] * b_t[:, None, :] * u_t[:, :, None]
            state = da * state + dbu
            y_t = jnp.einsum('bds,bs->bd', state, c_t)
            return (state, y_t)
        state0 = jnp.zeros((x.shape[0], D_INNER, D_STATE), dtype=x.dtype)
        to_t = lambda v: jnp.swapaxes(v, 0, 1)
        _, ys = lax.scan(step, state0, (to_t(xb), to_t(dt), to_t(b), to_t(c)))
        y = jnp.swapaxes(ys, 0, 1)
        y = (y + D_param * xb) * jax.nn.silu(z)
        return y @ out_proj_w

    def _L0_ffn_ref(x, wqkv, q_scale, k_scale, wo, ln_g, ln_b, w1, b1, w2, b2):
        import jax, jax.numpy as jnp
        import numpy as np
        DIM = 128
        DEPTH = 2
        HEADS = 8
        DIM_HEAD = 64
        WINDOW = 64
        INNER = HEADS * DIM_HEAD
        HID = int(DIM * 4 * 2 / 3)
        B, N = (2, 1024)
        QK_SCALE = 8.0

        def shift_token(t):
            t1, t2 = jnp.split(t, 2, axis=-1)
            t2 = jnp.pad(t2, ((0, 0), (1, 0), (0, 0)))[:, :-1]
            return jnp.concatenate([t1, t2], axis=-1)

        def l2norm(t):
            return t / jnp.clip(jnp.linalg.norm(t, axis=-1, keepdims=True), 1e-12)

        def rotate_half(x):
            x1, x2 = jnp.split(x, 2, axis=-1)
            return jnp.concatenate([-x2, x1], axis=-1)

        def rotary_xpos(q, k):
            n = q.shape[-2]
            half_idx = jnp.arange(0, DIM_HEAD, 2, dtype=jnp.float32)
            inv_freq = 1.0 / 10000.0 ** (half_idx / DIM_HEAD)
            t = jnp.arange(n, dtype=jnp.float32)
            freqs = t[:, None] * inv_freq[None, :]
            freqs = jnp.concatenate([freqs, freqs], axis=-1)
            base = (half_idx + 0.4 * DIM_HEAD) / (1.4 * DIM_HEAD)
            power = (t - n // 2) / float(WINDOW // 2)
            scale = base[None, :] ** power[:, None]
            scale = jnp.concatenate([scale, scale], axis=-1)
            cos, sin = (jnp.cos(freqs), jnp.sin(freqs))
            q = q * cos * scale + rotate_half(q) * sin * scale
            k = k * cos / scale + rotate_half(k) * sin / scale
            return (q, k)

        def local_attention(q, k, v):
            b, h, n, d = q.shape
            w = n // WINDOW
            bq = q.reshape(b, h, w, WINDOW, d) * QK_SCALE
            bk = k.reshape(b, h, w, WINDOW, d)
            bv = v.reshape(b, h, w, WINDOW, d)

            def look_around(t):
                p = jnp.pad(t, ((0, 0), (0, 0), (1, 0), (0, 0), (0, 0)))
                return jnp.concatenate([p[:, :, :w], p[:, :, 1:]], axis=3)
            bk, bv = (look_around(bk), look_around(bv))
            bt = jnp.arange(n).reshape(w, WINDOW)
            btp = jnp.pad(bt, ((1, 0), (0, 0)), constant_values=-1)
            btk = jnp.concatenate([btp[:w], btp[1:]], axis=1)
            sim = jnp.einsum('bhwid,bhwjd->bhwij', bq, bk)
            i = bt[:, :, None]
            j = btk[:, None, :]
            mask = (i < j) | (i > j + WINDOW) | (j == -1)
            sim = jnp.where(mask, -jnp.finfo(sim.dtype).max, sim)
            attn = jax.nn.softmax(sim, axis=-1)
            out = jnp.einsum('bhwij,bhwjd->bhwid', attn, bv)
            return out.reshape(b, h, n, d)

        def _layer(x, wqkv, qs, ksc, wo, lg, lb, w1, b1, w2, b2):
            b, n, _ = x.shape
            h = shift_token(x)
            qkv = h @ wqkv
            q, k, v = jnp.split(qkv, 3, axis=-1)
            to_heads = lambda t: t.reshape(b, n, HEADS, DIM_HEAD).transpose(0, 2, 1, 3)
            q, k, v = (to_heads(q), to_heads(k), to_heads(v))
            q = l2norm(q) * qs
            k = l2norm(k) * ksc
            q, k = rotary_xpos(q, k)
            o = local_attention(q, k, v)
            o = o.transpose(0, 2, 1, 3).reshape(b, n, INNER)
            x = x + o @ wo
            h = shift_token(x)
            mu = h.mean(-1, keepdims=True)
            var = h.var(-1, keepdims=True)
            h = (h - mu) / jnp.sqrt(var + 1e-05) * lg + lb
            h = h @ w1 + b1
            a, g = jnp.split(h, 2, axis=-1)
            h = a * jax.nn.gelu(g, approximate=False)
            x = x + h @ w2 + b2
            return x
        for l in range(DEPTH):
            x = _layer(x, wqkv[l], q_scale[l], k_scale[l], wo[l], ln_g[l], ln_b[l], w1[l], b1[l], w2[l], b2[l])
        return x
    x = L0_attn_x
    x = x + _layernorm(_L0_attn_ref(_layernorm(x, axis=-1), L0_attn_in_proj_w, L0_attn_conv_w, L0_attn_conv_b, L0_attn_x_proj_w, L0_attn_dt_proj_w, L0_attn_dt_proj_b, L0_attn_A_log, L0_attn_D_param, L0_attn_out_proj_w), axis=-1)
    x = x + _layernorm(_L0_ffn_ref(_layernorm(x, axis=-1), L0_ffn_wqkv, L0_ffn_q_scale, L0_ffn_k_scale, L0_ffn_wo, L0_ffn_ln_g, L0_ffn_ln_b, L0_ffn_w1, L0_ffn_b1, L0_ffn_w2, L0_ffn_b2), axis=-1)
    return x

_drawn_inputs = setup_inputs


def setup_inputs(seed=0):
    import zlib

    import numpy as np

    out = dict(_drawn_inputs(seed))
    spreads = {'L0_attn_D_param': (1.0, 0.2),
     'L0_ffn_q_scale': (1.0, 0.6),
     'L0_ffn_k_scale': (1.0, 0.6),
     'L0_ffn_ln_g': (1.0, 0.6),
     'L0_ffn_ln_b': (0.0, 0.8),
     'L0_ffn_b1': (0.0, 0.8),
     'L0_ffn_b2': (0.0, 0.8)}
    factors = {'L0_ffn_wqkv': 4.439, 'L0_ffn_wo': 4.348, 'L0_ffn_w1': 7.525, 'L0_ffn_w2': 7.414}
    for name, (base, spread) in spreads.items():
        noise = np.random.default_rng([zlib.crc32(name.encode()), seed]).standard_normal(out[name].shape)
        drawn = base * np.exp(spread * noise) if base else spread * noise
        out[name] = jnp.asarray(drawn.astype(out[name].dtype))
    for name, factor in factors.items():
        out[name] = (out[name] * factor).astype(out[name].dtype)
    return out
```

```python
from contextlib import ExitStack

import numpy as np

import concourse.bass as bass
from concourse import mybir

F32 = mybir.dt.float32
BF16 = mybir.dt.bfloat16
I32 = mybir.dt.int32
ALU = mybir.AluOpType
ACT = mybir.ActivationFunctionType
AX = mybir.AxisListType.X

B, T, D = 16, 512, 128
P = 128
NT = T // P
DI, NH2 = 256, 2
NS, NCONV, RANK = 16, 4, 8
DEPTH, HEADS, DH, WIN = 2, 8, 64, 64
INNER = HEADS * DH
NC = INNER // P
HID = 341
HCH = [(0, 128), (128, 128), (256, HID - 256)]
EPS = 1e-5
NEG = -1.0e30
MAGIC = 0x5F3759DF


class Op:

    def __init__(self, engine, run, after, cost, sem, step):
        self.engine, self.run, self.cost, self.sem, self.step = engine, run, cost, sem, step
        self.after = [a for a in after if a is not None]
        self.value = None
        for a in self.after:
            a.waited = True
        self.waited = step == 16


class Stage:

    def __init__(self, sems):
        self.sems, self.ops = sems, []

    def add(self, engine, run, *after, cost=None, dma=None):
        cost = cost if cost is not None else {"pe": 0.3, "sp": 0.0}.get(engine, 0.6)
        self.ops.append(Op(engine, run, after, cost, dma or self.sems[engine], 16 if dma else 1))
        return self.ops[-1]

    def pe(self, run, *after, **k):
        return self.add("pe", run, *after, **k)

    def act(self, run, *after, **k):
        return self.add("act", run, *after, **k)

    def dve(self, run, *after, **k):
        return self.add("dve", run, *after, **k)

    def pool(self, run, *after, **k):
        return self.add("pool", run, *after, **k)

    def sp(self, run, dma, *after, **k):
        return self.add("sp", run, *after, dma=dma, **k)


class Bank:

    def __init__(self, tile):
        self.t, self.readers = tile, []


def merged(stages, lead):
    keyed = []
    for n, s in enumerate(stages):
        total = sum(o.cost for o in s.ops)
        at = 0.0
        for k, o in enumerate(s.ops):
            keyed.append((lead[n] + (1 - lead[n]) * at / total, n, k, o))
            at += o.cost
    return [o for *_, o in sorted(keyed, key=lambda x: x[:3])]


def run_block(nc, ops, sems):
    count = {}
    for o in ops:
        if o.waited:
            count[o.sem.num] = count.get(o.sem.num, 0) + o.step
            o.value = count[o.sem.num]

    def program(name):
        def body(e):
            seen = {}
            for o in ops:
                if o.engine != name:
                    continue
                for a in o.after:
                    if seen.get(a.sem.num, 0) < a.value:
                        seen[a.sem.num] = a.value
                        e.wait_ge(a.sem, a.value)
                last = o.run(e)
                if o.waited:
                    last.then_inc(o.sem, o.step)
        return body

    with nc.Block() as block:
        block.sync(program("sp"))
        block.gpsimd(program("pool"))
        block.scalar(program("act"))
        block.vector(program("dve"))
        block.tensor(program("pe"))
    nc.all_engine_barrier()
    nums = sorted(s.num for s in sems)
    assert nums == list(range(nums[0], nums[0] + len(nums)))
    nc.sync.sem_clear(range(nums[0], nums[-1] + 1))
    nc.all_engine_barrier()


def bcast(ap, shape):
    return ap.to_broadcast(shape)


def build(nc, a, out):
    with ExitStack() as ctx:
        def sb(name, shape, dt=F32):
            return ctx.enter_context(nc.sbuf_tensor(name, shape, dt))

        def sem(name):
            return ctx.enter_context(nc.semaphore(name))

        engines = ("pe", "act", "dve", "pool", "sp")
        m_sems = {e: sem(f"mamba_{e}") for e in engines}
        l_sems = {e: sem(f"layers_{e}") for e in engines}
        s_x = sem("x_loaded")
        s_w = sem("weights_loaded")
        s_out = sem("out_stored")
        s_vs = [sem(f"v_shifted_{n}") for n in range(DEPTH * 2)]
        round_sems = [*m_sems.values(), *l_sems.values(), s_x, s_w, s_out, *s_vs]

        mb = [Bank(ctx.enter_context(nc.psum_tensor(f"m_bank{n}", [P, T], F32))) for n in range(4)]
        lb = [Bank(ctx.enter_context(nc.psum_tensor(f"l_bank{n}", [P, T], F32))) for n in range(4)]

        ident = sb("ident", [P, P])
        identb = sb("identb", [P, P], BF16)
        shift = sb("shift", [P, 2, P])
        selb = sb("selb", [96, 2 * NS, P], BF16)
        maskb = sb("maskb", [P, NT * P], BF16)
        half = sb("half", [P, NT])
        w_in = sb("w_in", [P, 2 * DI])
        conv_w = sb("conv_w", [P, NH2, NCONV])
        conv_b = sb("conv_b", [P, NH2])
        w_x = sb("w_x", [P, NH2, RANK + 2 * NS])
        w_dt = sb("w_dt", [2 * NS + RANK, DI])
        dt_b = sb("dt_b", [P, NH2])
        a_neg = sb("a_neg", [P, NH2, NS])
        d_par = sb("d_par", [P, NH2])
        w_out = sb("w_out", [P, NH2, D])
        wqkv = sb("wqkv", [P, DEPTH, 3 * INNER])
        wo = sb("wo", [P, DEPTH, NC, D])
        ln_g = sb("ln_g", [P, DEPTH])
        ln_b = sb("ln_b", [P, DEPTH])
        w1 = sb("w1", [P, DEPTH, 2 * HID])
        b1 = sb("b1", [P, DEPTH, 6])
        w2 = sb("w2", [P, DEPTH, 3, D])
        tab = sb("tab", [P, DEPTH, 4, NT, DH])
        scl = sb("scl", [P, DEPTH, 4, DH])
        a_log = sb("a_log", [P, NH2, NS])

        x_in = sb("x_in", [P, NT, D])
        m_stat = sb("m_stat", [P, NT, 6])
        m_mv = sb("m_mv", [P, NT, 2])
        m_ve = sb("m_ve", [P, NT])
        m_rs = sb("m_rs", [P, NT])
        m_xn = sb("m_xn", [P, NT, D])
        xn_t = sb("xn_t", [P, T])
        x_pad = sb("x_pad", [P, NH2, NCONV - 1 + T])
        cv = sb("cv", [P, NH2, T])
        u = sb("u", [P, NH2, T])
        zs = sb("zs", [P, NH2, T])
        bc3 = sb("bc3", [96, T], BF16)
        bc_r1 = sb("bc_r1", [32, T])
        bc_mid = sb("bc_mid", [32, T], BF16)
        dt_r = sb("dt_r", [2 * NS + RANK, T])
        dt_abs = cv
        dt = sb("dt", [P, NH2, T])
        du = sb("du", [P, NH2, T])
        da = sb("da", [P, 2, NH2, T])
        dbu = sb("dbu", [P, NH2, T])
        hs = sb("hs", [P, 2, NH2, T])
        cs = sb("cs", [P, 2, T])
        gy = sb("gy", [P, 2, NH2, T])
        yg = cv
        x_next = sb("x_next", [P, NT, D])

        x_cur = sb("x_cur", [P, NT, D])
        xa = sb("xa", [P, NT, D])
        l_stat = sb("l_stat", [P, NT, 6])
        l_mv = sb("l_mv", [P, NT, 2])
        l_ve = sb("l_ve", [P, NT])
        l_rs = sb("l_rs", [P, NT])
        h_t = sb("h_t", [P, T])
        sq = sb("sq", [P, 2, INNER])
        ss = sb("ss", [P, NT, 2, HEADS])
        rn = sb("rn", [P, NT, 2, HEADS])
        rn_t = sb("rn_t", [P, NT, 2, HEADS])
        rq8 = sb("rq8", [P, NT, HEADS])
        m1 = sb("m1", [P, 2, INNER])
        m2 = sb("m2", [P, 2, INNER])
        qr = sb("qr", [P, NT, INNER])
        kr = sb("kr", [P, NT, INNER])
        v = sb("v", [P, NT, HEADS, DH + 1])
        vs = sb("vs", [P, NT, HEADS, DH + 1])
        q_t = sb("q_t", [P, NC, T])
        rot = q_t[:, 0:2, :].rearrange("p c (a t d) -> p (c a) t d", a=2, t=NT)
        k_t = sb("k_t", [P, NC, WIN + T])
        mx = sb("mx", [P, HEADS, NT])
        nb = sb("nb", [P, HEADS, NT])
        pr = m1[:, :, :].rearrange("p b (t k) -> p b t k", t=NT)
        p_t = m2
        rd = sb("rd", [P, HEADS, NT])
        o = qr
        o_t = q_t
        h2 = sb("h2", [P, NT, D])
        h2n = sb("h2n", [P, NT, D])
        h2_t = sb("h2_t", [P, T])
        ge = sb("ge", [P, 2, T])
        ff = sb("ff", [P, 3, T])
        o_buf = sb("o_buf", [P, NT, D])

        def load(s):
            loads = [
                (ident[:, :], a["c_ident"]),
                (shift[:, :, :], a["c_shift"].rearrange("a p n -> p a n")),
                (gy[0:96, 0, :, :].rearrange("p a b -> p (a b)"), a["c_sel"][:, 0:1024]),
                (gy[0:96, 1, :, :].rearrange("p a b -> p (a b)"), a["c_sel"][:, 1024:2048]),
                (hs[0:96, 0, :, :].rearrange("p a b -> p (a b)"), a["c_sel"][:, 2048:3072]),
                (hs[0:96, 1, :, :].rearrange("p a b -> p (a b)"), a["c_sel"][:, 3072:4096]),
                (cs[:, 0, :], a["c_mask"]),
                (w_in[:, :], a["L0_attn_in_proj_w"]),
                (w_x[:, :, 0:2 * NS], a["L0_attn_x_proj_w"][:, RANK:].rearrange("(h p) n -> p h n", p=P)),
                (w_x[:, :, 2 * NS:], a["L0_attn_x_proj_w"][:, 0:RANK].rearrange("(h p) n -> p h n", p=P)),
                (w_dt[2 * NS:, :], a["L0_attn_dt_proj_w"]),
                (w_out[:, :, :], a["L0_attn_out_proj_w"].rearrange("(h p) n -> p h n", p=P)),
                (conv_w[:, :, :], a["L0_attn_conv_w"].rearrange("(h p) k -> p h k", p=P)),
                (a_log[:, :, :], a["L0_attn_A_log"].rearrange("(h p) k -> p h k", p=P)),
                (wqkv[:, :, :], a["L0_ffn_wqkv"].rearrange("l p n -> p l n")),
                (w1[:, :, :], a["L0_ffn_w1"].rearrange("l p n -> p l n")),
                *((rot[:, q, :, :], a["c_rot"][q, :, :].rearrange("(t p) d -> p t d", p=P)) for q in range(4)),
            ]
            for dst, name in ((conv_b, "L0_attn_conv_b"), (dt_b, "L0_attn_dt_proj_b"), (d_par, "L0_attn_D_param")):
                loads.append((dst[:, :], a[name].rearrange("(h p) -> p h", p=P)))
            for dst, name in ((ln_g, "L0_ffn_ln_g"), (ln_b, "L0_ffn_ln_b")):
                loads.append((dst[:, :], a[name].rearrange("l p -> p l")))
            for l in range(DEPTH):
                loads.append((wo[:, l, :, :], a["L0_ffn_wo"][l, :, :].rearrange("(c p) n -> p c n", p=P)))
                for c, (c0, n) in enumerate(HCH):
                    loads.append((w2[0:n, l, c, :], a["L0_ffn_w2"][l, c0:c0 + n, :]))
                    for g in range(2):
                        src = a["L0_ffn_b1"][l:l + 1, g * HID + c0:g * HID + c0 + n]
                        loads.append((b1[0:n, l, 3 * g + c:3 * g + c + 1], src.rearrange("a p -> p a")))
                loads.append((w2[n:n + 1, l, 2, :], a["L0_ffn_b2"][l:l + 1, :]))
                for q, name in ((0, "L0_ffn_q_scale"), (2, "L0_ffn_k_scale")):
                    src = a[name][l:l + 1, :]
                    hd = DH // 2
                    for dst, piece in ((scl[:, l, q, :], src), (scl[:, l, q + 1, 0:hd], src[:, hd:DH]),
                                       (scl[:, l, q + 1, hd:DH], src[:, 0:hd])):
                        loads.append((dst, piece.to_broadcast([P, piece.shape[1]])))
            for n, (dst, src) in enumerate(loads):
                w = s.sp(lambda e, d=dst, r=src: e.dma_start(d, r, allow_slow_non_contiguous=True), s_w)
            s.dve(lambda e: e.memset(half[:, :], -0.5))
            s.dve(lambda e: e.memset(x_pad[:, :, 0:NCONV - 1], 0.0))
            s.dve(lambda e: e.memset(h_t[DH:, 0:1], 0.0))
            s.dve(lambda e: e.memset(k_t[:, :, 0:WIN], 0.0))
            s.dve(lambda e: e.memset(v[:, :, :, :], 1.0))
            s.dve(lambda e: e.memset(vs[0:WIN, 0, :, :], 0.0))
            s.dve(lambda e: e.memset(ff[:, 2, :], 1.0))
            s.dve(lambda e: e.tensor_copy(identb[:, :], ident[:, :]), w)
            s.dve(lambda e: e.tensor_copy(selb[:, 0:8, :].rearrange("p a b -> p (a b)"), gy[0:96, 0, :, :].rearrange("p a b -> p (a b)")), w)
            s.dve(lambda e: e.tensor_copy(selb[:, 8:16, :].rearrange("p a b -> p (a b)"), gy[0:96, 1, :, :].rearrange("p a b -> p (a b)")), w)
            s.dve(lambda e: e.tensor_copy(selb[:, 16:24, :].rearrange("p a b -> p (a b)"), hs[0:96, 0, :, :].rearrange("p a b -> p (a b)")), w)
            s.dve(lambda e: e.tensor_copy(selb[:, 24:32, :].rearrange("p a b -> p (a b)"), hs[0:96, 1, :, :].rearrange("p a b -> p (a b)")), w)
            s.dve(lambda e: e.tensor_copy(maskb[:, :], cs[:, 0, :]), w)
            for l in range(DEPTH):
                for q in range(4):
                    s.dve(lambda e, l=l, q=q: e.tensor_tensor(
                        tab[:, l, q, :, :], rot[:, q, :, :], bcast(scl[:, l, q:q + 1, :], [P, NT, DH]), ALU.mult), w)
            ex = s.act(lambda e: e.activation(a_neg[:, :, :], a_log[:, :, :], ACT.Exp), w)
            s.dve(lambda e: e.tensor_scalar(a_neg[:, :, :], a_neg[:, :, :], -1.0, None, ALU.mult), ex)

        def norm_scale(s, src, st, mv, ve, rs, *after):
            n = None
            for t in range(NT):
                n = s.dve(lambda e, t=t: e.bn_stats(st[:, t, :], src(t)), *after, cost=0.2)
            for t in range(NT):
                n2 = s.dve(lambda e, t=t: e.bn_aggr(mv[:, t, :], st[:, t, :]), n, cost=0.1)
            n3 = s.dve(lambda e: e.tensor_scalar(ve[:, :], mv[:, :, 1], EPS, None, ALU.add), n2, cost=0.1)
            return s.pool(lambda e: e.tensor_tensor(rs[:, :], ve[:, :], half[:, :], ALU.pow), n3, cost=1)

        def normalise(s, dst, src, mv, rs, *after):
            for t in range(NT):
                n = s.dve(lambda e, t=t: e.tensor_scalar(dst(t), src(t), mv[:, t, 0:1], rs[:, t:t + 1],
                                                         ALU.subtract, ALU.mult), *after, cost=0.2)
            return n

        def transposes(s, bank, src, *after):
            for n in range(4):
                last = s.pe(lambda e, n=n: e.transpose(bank.t[:, n * P:(n + 1) * P], src(n), ident[:, :]),
                            *after, *bank.readers, cost=0.11)
            return last

        def mamba(s, b, x_next_free):
            B0, B1, B2, B3 = mb
            for k in mb:
                k.readers = []
            ld = s.sp(lambda e: e.dma_start(x_in[:, :, :], a["L0_attn_x"][bass.ds(b, 1), :, :].rearrange(
                "b (t p) d -> p (b t) d", p=P)), s_x)
            rs = norm_scale(s, lambda t: x_in[:, t, :], m_stat, m_mv, m_ve, m_rs, ld)
            xn = normalise(s, lambda t: m_xn[:, t, :], lambda t: x_in[:, t, :], m_mv, m_rs, rs)
            tr = transposes(s, B0, lambda n: m_xn[:, n, :], xn)
            xt = s.act(lambda e: e.activation(xn_t[:, :], B0.t[:, :], ACT.Copy), tr)
            B0.readers = [xt]
            proj = []
            for c, bank in enumerate((B1, B2, B3, B0)):
                proj.append(s.pe(lambda e, c=c, bank=bank: e.matmul(
                    bank.t[:, :], w_in[:, c * P:(c + 1) * P], xn_t[:, :], start=True, stop=True),
                    xt, *bank.readers, cost=0.85))
            cv_done = []
            for h, bank in enumerate((B1, B2)):
                cp = s.act(lambda e, h=h, bank=bank: e.activation(
                    x_pad[:, h, NCONV - 1:], bank.t[:, :], ACT.Copy), proj[h])
                bank.readers = [cp]
                n = s.dve(lambda e, h=h: e.tensor_scalar(
                    cv[:, h, :], x_pad[:, h, NCONV - 1:], conv_w[:, h, NCONV - 1:NCONV], conv_b[:, h:h + 1],
                    ALU.mult, ALU.add), cp)
                for k in range(NCONV - 1):
                    n = s.dve(lambda e, h=h, k=k: e.scalar_tensor_tensor(
                        cv[:, h, :], x_pad[:, h, k:k + T], conv_w[:, h, k:k + 1], cv[:, h, :],
                        ALU.mult, ALU.add), n)
                cv_done.append(n)
            for h, bank in enumerate((B3, B0)):
                bank.readers = [s.act(lambda e, h=h, bank=bank: e.activation(zs[:, h, :], bank.t[:, :], ACT.Silu),
                                      proj[2 + h])]
            for h in range(NH2):
                us = s.act(lambda e, h=h: e.activation(u[:, h, :], cv[:, h, :], ACT.Silu), cv_done[h])
            for h in range(NH2):
                xp = s.pe(lambda e, h=h: e.matmul(B1.t[0:2 * NS + RANK, :], w_x[:, h, :], u[:, h, :],
                                                  start=h == 0, stop=h == 1), us, *B1.readers, cost=0.85)
            hi = s.act(lambda e: e.activation(bc3[0:32, :], B1.t[0:32, :], ACT.Copy), xp)
            dr = s.act(lambda e: e.activation(dt_r[32:40, :], B1.t[32:40, :], ACT.Copy), xp)
            r1 = s.dve(lambda e: e.tensor_tensor(bc_r1[:, :], B1.t[0:32, :], bc3[0:32, :], ALU.subtract),
                       hi, dr)
            B1.readers = [r1]
            mid = s.dve(lambda e: e.tensor_copy(bc_mid[:, :], bc_r1[:, :]), r1)
            mid3 = s.act(lambda e: e.activation(bc3[32:64, :], bc_r1[:, :], ACT.Copy), r1)
            lo = s.dve(lambda e: e.tensor_tensor(bc3[64:96, :], bc_r1[:, :], bc_mid[:, :], ALU.subtract), mid)
            dts = []
            for h, bank in enumerate((B2, B3)):
                dp = s.pe(lambda e, h=h, bank=bank: e.matmul(
                    bank.t[:, :], w_dt[32:40, h * P:(h + 1) * P], dt_r[32:40, :], start=True, stop=True),
                    dr, *bank.readers, cost=0.85)
                ab = s.act(lambda e, h=h, bank=bank: e.activation(
                    dt_abs[:, h, :], bank.t[:, :], ACT.Abs, bias=dt_b[:, h:h + 1]), dp)
                rl = s.dve(lambda e, h=h, bank=bank: e.tensor_scalar(
                    dt[:, h, :], bank.t[:, :], dt_b[:, h:h + 1], 0.0, ALU.add, ALU.max), ab)
                bank.readers = [rl]
                dts.append((ab, rl))
            exs = [s.act(lambda e, h=h: e.activation(dt_abs[:, h, :], dt_abs[:, h, :], ACT.Exp, scale=-1.0), dts[h][0])
                   for h in range(NH2)]
            lns = [s.act(lambda e, h=h: e.activation(dt_abs[:, h, :], dt_abs[:, h, :], ACT.Ln, bias=1.0), exs[h])
                   for h in range(NH2)]
            for h in range(NH2):
                dd = s.dve(lambda e, h=h: e.tensor_tensor(dt[:, h, :], dt[:, h, :], dt_abs[:, h, :], ALU.add),
                           lns[h], dts[h][1])
                dudone = s.dve(lambda e, h=h: e.tensor_tensor(du[:, h, :], dt[:, h, :], u[:, h, :], ALU.mult), dd)
            acc = (B0, B1)
            das, scans, gs, ys = {}, {}, {}, {}

            def sum_state(n):
                for h in range(NH2):
                    ys[n, h] = s.pe(lambda e, h=h: e.matmul(
                        acc[h].t[:, :], ident[:, :], gy[:, n % 2, h, :], start=n == 0, stop=n == NS - 1),
                        gs[n, h], *(acc[h].readers if n == 0 else []), cost=0.85)

            cscp = {}
            for n in range(NS):
                j = n % 2
                bb = s.pe(lambda e, n=n: e.matmul(B2.t[:, :], selb[:, n, :], bc3[:, :], start=True, stop=True),
                          hi, mid3, lo, *B2.readers, cost=0.22)
                cc = s.pe(lambda e, n=n: e.matmul(B3.t[:, :], selb[:, NS + n, :], bc3[:, :], start=True, stop=True),
                          *B3.readers, cost=0.22)
                for h in range(NH2):
                    das[n, h] = s.act(lambda e, n=n, h=h, j=j: e.activation(
                        da[:, j, h, :], dt[:, h, :], ACT.Exp, scale=a_neg[:, h, n:n + 1]),
                        dd, scans.get((n - 2, h)))
                cscp[n] = s.act(lambda e, j=j: e.activation(cs[:, j, :], B3.t[:, :], ACT.Copy),
                                cc, gs.get((n - 2, 1)))
                B3.readers = [cscp[n]]
                for h in range(NH2):
                    db = s.dve(lambda e, h=h: e.tensor_tensor(dbu[:, h, :], du[:, h, :], B2.t[:, :], ALU.mult),
                               bb, dudone)
                    scans[n, h] = s.dve(lambda e, h=h, j=j: e.tensor_tensor_scan(
                        hs[:, j, h, :], da[:, j, h, :], dbu[:, h, :], 0.0, ALU.mult, ALU.add),
                        db, das[n, h], gs.get((n - 2, h)))
                B2.readers = [db]
                for h in range(NH2):
                    gs[n, h] = s.pool(lambda e, h=h, j=j: e.tensor_tensor(
                        gy[:, j, h, :], hs[:, j, h, :], cs[:, j, :], ALU.mult),
                        scans[n, h], cscp[n], ys.get((n - 2, h)), cost=1.2)
                if n:
                    sum_state(n - 1)
            sum_state(NS - 1)
            for h in range(NH2):
                yd = s.dve(lambda e, h=h: e.scalar_tensor_tensor(
                    yg[:, h, :], u[:, h, :], d_par[:, h:h + 1], acc[h].t[:, :], ALU.mult, ALU.add), ys[NS - 1, h])
                acc[h].readers = [yd]
                yz = s.dve(lambda e, h=h: e.tensor_tensor(yg[:, h, :], yg[:, h, :], zs[:, h, :], ALU.mult), yd)
            for t in range(NT):
                for h in range(NH2):
                    op = s.pe(lambda e, t=t, h=h: e.matmul(
                        B2.t[:, t * P:(t + 1) * P], yg[:, h, t * P:(t + 1) * P], w_out[:, h, :],
                        start=h == 0, stop=h == 1), yz, *B2.readers, cost=0.21)
            rs = norm_scale(s, lambda t: B2.t[:, t * P:(t + 1) * P], m_stat, m_mv, m_ve, m_rs, op)
            xn = normalise(s, lambda t: m_xn[:, t, :], lambda t: B2.t[:, t * P:(t + 1) * P], m_mv, m_rs, rs)
            s.dve(lambda e: e.tensor_tensor(x_next[:, :, :], m_xn[:, :, :], x_in[:, :, :], ALU.add),
                  xn, x_next_free)

        def layers(s, b):
            for k in lb:
                k.readers = []
            L0, L1, L2, L3 = lb
            first = s.dve(lambda e: e.tensor_copy(x_cur[:, :, :], x_next[:, :, :]))
            rs = norm_scale(s, lambda t: x_cur[:, t, :], l_stat, l_mv, l_ve, l_rs, first)
            x_done = normalise(s, lambda t: xa[:, t, :], lambda t: x_cur[:, t, :], l_mv, l_rs, rs)
            for l in range(DEPTH):
                x_done = layer(s, l, x_done)
            rs = norm_scale(s, lambda t: xa[:, t, :], l_stat, l_mv, l_ve, l_rs, x_done)
            xn = normalise(s, lambda t: xa[:, t, :], lambda t: xa[:, t, :], l_mv, l_rs, rs)
            wr = s.dve(lambda e: e.tensor_tensor(o_buf[:, :, :], xa[:, :, :], x_cur[:, :, :], ALU.add), xn)
            store = s.sp(lambda e: e.dma_start(out[bass.ds(b, 1), :, :].rearrange(
                "b (t p) d -> p (b t) d", p=P), o_buf[:, :, :]), s_out, wr)
            s.add("sp", lambda e: None, store)
            return first

        def layer(s, l, x_done):
            L0, L1, L2, L3 = lb
            tr = transposes(s, L0, lambda n: xa[:, n, :], x_done)
            c0 = s.act(lambda e: e.activation(h_t[0:DH, :], L0.t[0:DH, :], ACT.Copy), tr)
            c1 = s.act(lambda e: e.activation(h_t[DH:, 1:T], L0.t[DH:, 0:T - 1], ACT.Copy), tr)
            L0.readers = [c1]
            ring, at = [L1, L2, L3, L0], 0
            sq_read = {}
            m_read = {}
            added = {0: [], 1: []}
            for t in range(NT):
                for part in range(3):
                    bank = ring[at % 4]
                    at += 1
                    mm = s.pe(lambda e, t=t, part=part, bank=bank: e.matmul(
                        bank.t[:, :], h_t[:, t * P:(t + 1) * P], wqkv[:, l, part * INNER:(part + 1) * INNER],
                        start=True, stop=True), c0, c1, *bank.readers, cost=0.85)
                    if part == 2:
                        vc = s.act(lambda e, t=t, bank=bank: e.activation(
                            v[:, t, :, 0:DH], bank.t[:, :].rearrange("p (h d) -> p h d", h=HEADS), ACT.Copy), mm)
                        bank.readers = [vc]
                        continue
                    sqd = s.act(lambda e, part=part, bank=bank: e.activation(sq[:, part, :], bank.t[:, :], ACT.Square),
                                mm, sq_read.get(part))
                    sq_read[part] = red = s.dve(lambda e, t=t, part=part: e.tensor_reduce(
                        ss[:, t, part, :], sq[:, part, :].rearrange("p (h d) -> p h d", h=HEADS), AX, ALU.add), sqd)
                    q4 = bank.t[:, :].rearrange("p (h a d) -> p h a d", h=HEADS, a=2)

                    def table(n, t=t):
                        return bcast(tab[:, l, n, t:t + 1, :], [P, HEADS, DH]).rearrange("p h (a d) -> p h a d", a=2)
                    ma = s.dve(lambda e, q4=q4, part=part, tb=table(2 * part): e.tensor_tensor(
                        m1[:, part, :].rearrange("p (h a d) -> p h a d", h=HEADS, a=2), q4, tb, ALU.mult),
                        sqd, m_read.get(part))
                    mc = s.dve(lambda e, q4=q4, part=part, tb=table(2 * part + 1): e.tensor_tensor(
                        m2[:, part, :].rearrange("p (h a d) -> p h a d", h=HEADS, a=2), q4[:, :, ::-1, :], tb,
                        ALU.mult), sqd)
                    bank.readers = [mc]
                    dst = (qr, kr)[part]
                    m_read[part] = ad = s.pool(lambda e, t=t, part=part, dst=dst: e.tensor_tensor(
                        dst[:, t, :], m1[:, part, :], m2[:, part, :], ALU.add), mc, cost=1.2)
                    added[part].append(ad)
            v1 = s.sp(lambda e: e.dma_start(vs[0:WIN, 1:NT, :, :], v[WIN:, 0:NT - 1, :, :]), s_vs[2 * l], vc)
            v2 = s.sp(lambda e: e.dma_start(vs[WIN:, :, :, :], v[0:WIN, :, :, :]), s_vs[2 * l + 1], vc)
            flat = lambda x: x[:, :, :, :].rearrange("p t a h -> p (t a h)")
            n = s.dve(lambda e: e.tensor_scalar(flat(ss), flat(ss), 1e-24, None, ALU.max), red, cost=0.13)
            n = s.dve(lambda e: e.tensor_single_scalar(flat(rn_t).bitcast(I32), flat(ss).bitcast(I32), 1,
                                                       ALU.arith_shift_right), n, cost=0.13)
            n = s.dve(lambda e: e.tensor_scalar(flat(rn).bitcast(I32), flat(rn_t).bitcast(I32), -1.0, float(MAGIC),
                                                ALU.mult, ALU.add), n, cost=0.13)
            for _ in range(3):
                n = s.dve(lambda e: e.scalar_tensor_tensor(flat(rn_t), flat(ss), -0.5, flat(rn), ALU.mult, ALU.mult),
                          n, cost=0.13)
                n = s.dve(lambda e: e.tensor_tensor(flat(rn_t), flat(rn_t), flat(rn), ALU.mult), n, cost=0.13)
                n = s.dve(lambda e: e.scalar_tensor_tensor(flat(rn), flat(rn_t), 1.5, flat(rn), ALU.add, ALU.mult),
                          n, cost=0.13)
            q8 = s.dve(lambda e: e.tensor_scalar(rq8[:, :, :], rn[:, :, 0, :], 8.0, None, ALU.mult), n, cost=0.1)
            for t in range(NT):
                kn = s.dve(lambda e, t=t: e.tensor_tensor(
                    kr[:, t, :].rearrange("p (h d) -> p h d", h=HEADS), kr[:, t, :].rearrange("p (h d) -> p h d", h=HEADS),
                    bcast(rn[:, t, 1, :].unsqueeze(2), [P, HEADS, DH]), ALU.mult), n, added[1][t])
            qt, kt = {}, {}
            for c in range(NC):
                for dst, src, w, done in ((q_t, qr, added[0][-1], qt), (k_t, kr, kn, kt)):
                    bank = ring[at % 4]
                    at += 1
                    tr = transposes(s, bank, lambda n, c=c, src=src: src[:, n, c * P:(c + 1) * P], w)
                    off = T if dst is q_t else WIN + T
                    done[c] = s.act(lambda e, c=c, dst=dst, off=off, bank=bank: e.activation(
                        dst[:, c, off - T:off], bank.t[:, :], ACT.Copy), tr)
                    bank.readers = [done[c]]
            sc, exps, pts, avs, o_done = {}, {}, {}, {}, {}
            s_bank = lambda h: (L0, L1)[h % 2]

            def scores(hd):
                c, r = hd // 2, DH * (hd % 2)
                bank = s_bank(hd)
                s.pe(lambda e: e.matmul(bank.t[:, :], identb[:, :], maskb[:, :], start=True, stop=False,
                                        skip_group_check=True), *bank.readers, cost=0.22)
                for p in range(NT):
                    for j in range(2):
                        sc[hd] = s.pe(lambda e, p=p, j=j: e.matmul(
                            bank.t[WIN * j:WIN * j + WIN, p * P:(p + 1) * P],
                            q_t[r:r + DH, c, p * P + WIN * j:p * P + WIN * j + WIN],
                            k_t[r:r + DH, c, p * P + WIN * j:p * P + WIN * j + P],
                            start=False, stop=True, skip_group_check=True), qt[c], kt[c], cost=0.15)

            scores(0)
            for hd in range(HEADS):
                j2 = hd % 2
                if hd + 1 < HEADS:
                    scores(hd + 1)
                bank = s_bank(hd)
                mxd = s.dve(lambda e, hd=hd, bank=bank: e.tensor_reduce(
                    mx[:, hd, :], bank.t[:, :].rearrange("p (t k) -> p t k", t=NT), AX, ALU.max), sc[hd])
                nbd = s.dve(lambda e, hd=hd: e.scalar_tensor_tensor(
                    nb[:, hd, :], mx[:, hd, :], -1.0, rq8[:, :, hd], ALU.mult, ALU.mult), mxd, q8, cost=0.1)
                for p in range(NT):
                    exps[hd] = s.act(lambda e, hd=hd, p=p, bank=bank, j2=j2: e.activation(
                        pr[:, j2, p, :], bank.t[:, p * P:(p + 1) * P], ACT.Exp, bias=nb[:, hd, p:p + 1],
                        scale=rq8[:, p, hd:hd + 1]), nbd, pts.get(hd - 2), cost=0.35)
                bank.readers = [exps[hd]]
                pts[hd] = tr = transposes(s, L2, lambda n, j2=j2: pr[:, j2, n, :], exps[hd])
                if hd % 2:
                    pc = s.dve(lambda e, j2=j2: e.tensor_copy(p_t[:, j2, :], L2.t[:, :]), tr, avs.get(hd - 2))
                else:
                    pc = s.act(lambda e, j2=j2: e.activation(p_t[:, j2, :], L2.t[:, :], ACT.Copy), tr, avs.get(hd - 2))
                L2.readers = [pc]
                ot = L3.t[:, 0:NT * (DH + 1)].rearrange("p (t d) -> p t d", t=NT)
                for p in range(NT):
                    for j in range(2):
                        avs[hd] = s.pe(lambda e, hd=hd, p=p, j=j, j2=j2, ot=ot: e.matmul(
                            ot[WIN * j:WIN * j + WIN, p, :],
                            p_t[:, j2, p * P + WIN * j:p * P + WIN * j + WIN],
                            (vs, v)[j][:, p, hd, :], start=True, stop=True), pc, v1, v2, *L3.readers, cost=0.11)
                rc = s.dve(lambda e, hd=hd, ot=ot: e.reciprocal(rd[:, hd, :], ot[:, :, DH]), avs[hd], cost=0.12)
                od = s.dve(lambda e, hd=hd, ot=ot: e.tensor_tensor(
                    o[:, :, hd * DH:(hd + 1) * DH], ot[:, :, 0:DH],
                    bcast(rd[:, hd, :].unsqueeze(2), [P, NT, DH]), ALU.mult), rc, cost=0.33)
                L3.readers = [od]
            oc = {}
            for c in range(NC):
                bank = (L0, L1, L2, L0)[c]
                tr = transposes(s, bank, lambda n, c=c: o[:, n, c * P:(c + 1) * P], od)
                oc[c] = s.act(lambda e, c=c, bank=bank: e.activation(o_t[:, c, :], bank.t[:, :], ACT.Copy), tr)
                bank.readers = [oc[c]]
            for t in range(NT):
                for c in range(NC):
                    mm = s.pe(lambda e, t=t, c=c: e.matmul(
                        L3.t[:, t * P:(t + 1) * P], o_t[:, c, t * P:(t + 1) * P], wo[:, l, c, :],
                        start=c == 0, stop=c == NC - 1), oc[c], *L3.readers, cost=0.21)
            tm = lambda bank: bank.t[:, :].rearrange("p (t d) -> p t d", t=NT)
            x2 = s.dve(lambda e: e.tensor_tensor(xa[:, :, :], xa[:, :, :], tm(L3), ALU.add), mm)
            L3.readers = [x2]
            sh = L0.t[:, 0:NT * DH].rearrange("p (t d) -> p t d", t=NT)
            s.pe(lambda e: e.matmul(sh, shift[:, 0, :], xa[:, :, DH:], start=True, stop=False,
                                    skip_group_check=True), x2, *L0.readers, cost=0.43)
            mm = s.pe(lambda e: e.matmul(sh[:, 1:, :], shift[:, 1, :], xa[:, 0:NT - 1, DH:], start=False, stop=True,
                                         skip_group_check=True), cost=0.32)
            ha = s.pool(lambda e: e.tensor_copy(h2[:, :, 0:DH], xa[:, :, 0:DH]), x2)
            hb = s.act(lambda e: e.activation(h2[:, :, DH:], sh, ACT.Copy), mm, cost=0.35)
            L0.readers = [hb]
            rs = norm_scale(s, lambda t: h2[:, t, :], l_stat, l_mv, l_ve, l_rs, ha, hb)
            hn = normalise(s, lambda t: h2n[:, t, :], lambda t: h2[:, t, :], l_mv, l_rs, rs)
            tr = transposes(s, L1, lambda n: h2n[:, n, :], hn)
            ht = s.act(lambda e: e.activation(h2_t[:, :], L1.t[:, :], ACT.Identity, bias=ln_b[:, l:l + 1],
                                              scale=ln_g[:, l:l + 1]), tr)
            L1.readers = [ht]
            ge_read = {}
            for c, (c0_, n) in enumerate(HCH):
                ab, gb = ((L2, L3), (L0, L1), (L2, L3))[c]
                mg = s.pe(lambda e, c0_=c0_, n=n, gb=gb: e.matmul(
                    gb.t[0:n, :], w1[:, l, HID + c0_:HID + c0_ + n], h2_t[:, :], start=True, stop=True),
                    ht, *gb.readers, cost=0.85)
                ma = s.pe(lambda e, c0_=c0_, n=n, ab=ab: e.matmul(
                    ab.t[0:n, :], w1[:, l, c0_:c0_ + n], h2_t[:, :], start=True, stop=True),
                    ht, *ab.readers, cost=0.85)
                gd = s.act(lambda e, c=c, n=n, gb=gb: e.activation(
                    ge[0:n, c % 2, :], gb.t[0:n, :], ACT.Gelu, bias=b1[0:n, l, 3 + c:4 + c]), mg, ge_read.get(c % 2))
                gb.readers = [gd]
                ge_read[c % 2] = fd = s.dve(lambda e, c=c, n=n, ab=ab: e.scalar_tensor_tensor(
                    ff[0:n, c, :], ab.t[0:n, :], b1[0:n, l, c:c + 1], ge[0:n, c % 2, :], ALU.add, ALU.mult), ma, gd)
                ab.readers = [fd]
            for t in range(NT):
                for c, (c0_, n) in enumerate(HCH):
                    k = n + (c == 2)
                    mm = s.pe(lambda e, t=t, c=c, k=k: e.matmul(
                        L0.t[:, t * P:(t + 1) * P], ff[0:k, c, t * P:(t + 1) * P], w2[0:k, l, c, :],
                        start=c == 0, stop=c == 2), fd, *L0.readers, cost=0.21)
            x3 = s.dve(lambda e: e.tensor_tensor(xa[:, :, :], xa[:, :, :], tm(L0), ALU.add), mm)
            L0.readers = [x3]
            return x3

        s = Stage(m_sems)
        load(s)
        run_block(nc, s.ops, round_sems)

        s = Stage(m_sems)
        mamba(s, 0, None)
        run_block(nc, s.ops, round_sems)

        with nc.Fori(0, B - 1) as i:
            sl, sm = Stage(l_sems), Stage(m_sems)
            x_cur_copied = layers(sl, i)
            mamba(sm, i + 1, x_cur_copied)
            run_block(nc, merged([sl, sm], LEAD), round_sems)

        s = Stage(l_sems)
        layers(s, B - 1)
        run_block(nc, s.ops, round_sems)


LEAD = [0.0, 0.03]

_INS = ["L0_attn_x", "L0_attn_in_proj_w", "L0_attn_conv_w", "L0_attn_conv_b", "L0_attn_x_proj_w",
        "L0_attn_dt_proj_w", "L0_attn_dt_proj_b", "L0_attn_A_log", "L0_attn_D_param", "L0_attn_out_proj_w",
        "L0_ffn_wqkv", "L0_ffn_q_scale", "L0_ffn_k_scale", "L0_ffn_wo", "L0_ffn_ln_g", "L0_ffn_ln_b",
        "L0_ffn_w1", "L0_ffn_b1", "L0_ffn_w2", "L0_ffn_b2"]


def constants():
    f = np.float32
    c = {"c_ident": np.eye(P, dtype=f)}
    sh = np.zeros((2, P, P), f)
    sh[0, np.arange(P - 1), np.arange(1, P)] = 1
    sh[1, P - 1, 0] = 1
    c["c_shift"] = sh
    sel = np.zeros((96, 2 * NS, P), f)
    for part in range(3):
        for r in range(2 * NS):
            sel[32 * part + r, r, :] = 1
    c["c_sel"] = sel.reshape(96, 2 * NS * P)
    q, k = np.arange(P)[:, None], np.arange(P)[None, :]
    i = q % WIN
    bad = (i + WIN < k) | (i + WIN > k + WIN)
    m = np.zeros((P, NT, P), bool)
    m[:] = bad[:, None, :]
    m[0:WIN, 0, 0:WIN] = True
    c["c_mask"] = np.where(m, f(NEG), f(0)).reshape(P, NT * P)
    hi = np.arange(0, DH, 2, dtype=f)
    inv = f(1) / f(10000.0) ** (hi / f(DH))
    t = np.arange(T, dtype=f)
    fr = np.concatenate([t[:, None] * inv[None, :]] * 2, -1)
    base = (hi + f(0.4 * DH)) / f(1.4 * DH)
    power = (t - T // 2) / f(WIN // 2)
    sc = np.concatenate([base[None, :] ** power[:, None]] * 2, -1)
    sign = np.where(np.arange(DH) < DH // 2, f(-1), f(1))
    cos, sin = np.cos(fr), np.sin(fr) * sign
    c["c_rot"] = np.stack([cos * sc, sin * sc, cos / sc, sin / sc]).astype(f)
    return c


def kernel(**inputs):
    import concourse.bacc as _bacc
    from concourse.bass_utils import run_bass_kernel_spmd as _run

    nc = _bacc.Bacc("TRN2", target_bir_lowering=False, num_devices=1)
    arrays, aps = {}, {}
    for name, x in [*((n, inputs[n]) for n in _INS), *constants().items()]:
        x = np.ascontiguousarray(x)
        arrays[f"in_{name}"] = x
        aps[name] = nc.dram_tensor(f"in_{name}", x.shape, mybir.dt.from_np(x.dtype), kind="ExternalInput").ap()
    out = nc.dram_tensor("out_dram", (B, T, D), F32, kind="ExternalOutput").ap()
    build(nc, aps, out)
    r = _run(nc, [arrays], core_ids=[0])
    return r.results[0]["out_dram"]
```

```python
from contextlib import ExitStack

import numpy as np

import concourse.bass as bass
from concourse import mybir

F32 = mybir.dt.float32
BF16 = mybir.dt.bfloat16
I32 = mybir.dt.int32
ALU = mybir.AluOpType
ACT = mybir.ActivationFunctionType
AX = mybir.AxisListType.X

B, T, D = 16, 512, 128
P = 128
NT = T // P
DI, NH2 = 256, 2
NS, NCONV, RANK = 16, 4, 8
DEPTH, HEADS, DH, WIN = 2, 8, 64, 64
INNER = HEADS * DH
NC = INNER // P
HID = 341
HCH = [(0, 128), (128, 128), (256, HID - 256)]
EPS = 1e-5
NEG = -1.0e30
MAGIC = 0x5F3759DF


class Op:

    def __init__(self, engine, run, after, cost, sem, step):
        self.engine, self.run, self.cost, self.sem, self.step = engine, run, cost, sem, step
        self.after = [a for a in after if a is not None]
        self.value = None
        for a in self.after:
            a.waited = True
        self.waited = step == 16


class Stage:

    def __init__(self, sems):
        self.sems, self.ops = sems, []

    def add(self, engine, run, *after, cost=None, dma=None):
        cost = cost if cost is not None else {"pe": 0.85, "act": 0.48, "dve": 0.6, "pool": 1.22, "sp": 0.0}[engine]
        self.ops.append(Op(engine, run, after, cost, dma or self.sems[engine], 16 if dma else 1))
        return self.ops[-1]

    def pe(self, run, *after, **k):
        return self.add("pe", run, *after, **k)

    def act(self, run, *after, **k):
        return self.add("act", run, *after, **k)

    def dve(self, run, *after, **k):
        return self.add("dve", run, *after, **k)

    def pool(self, run, *after, **k):
        return self.add("pool", run, *after, **k)

    def sp(self, run, dma, *after, **k):
        return self.add("sp", run, *after, dma=dma, **k)


class Bank:

    def __init__(self, tile):
        self.t, self.readers = tile, []


LATENCY = {"pe": 0.2, "act": 0.25, "dve": 0.15, "pool": 0.2, "sp": 2.0}


def merged(stages):
    queues = [{e: [o for o in s.ops if o.engine == e] for e in LATENCY} for s in stages]
    heads = [dict.fromkeys(LATENCY, 0) for _ in stages]
    left = [sum(o.cost for o in s.ops) for s in stages]
    free, end, order = dict.fromkeys(LATENCY, 0.0), {}, []
    while True:
        best = None
        for n, q in enumerate(queues):
            for e in LATENCY:
                if heads[n][e] == len(q[e]):
                    continue
                o = q[e][heads[n][e]]
                if any(id(x) not in end for x in o.after):
                    continue
                start = max([free[e]] + [end[id(x)] + LATENCY[x.engine] for x in o.after])
                key = (start, n not in FIRST, -left[n], n, e)
                if best is None or key < best[0]:
                    best = (key, o, start)
        if best is None:
            break
        (_, _, _, n, e), o, start = best
        heads[n][e] += 1
        left[n] -= o.cost
        free[e] = start + (0.05 if e == "sp" else o.cost)
        end[id(o)] = start + o.cost
        order.append(o)
    assert len(order) == sum(len(s.ops) for s in stages)
    return order


FIRST = ()


def run_block(nc, ops, sems):
    count = {}
    for o in ops:
        if o.waited:
            count[o.sem.num] = count.get(o.sem.num, 0) + o.step
            o.value = count[o.sem.num]

    def program(name):
        def body(e):
            seen = {}
            for o in ops:
                if o.engine != name:
                    continue
                for a in o.after:
                    if seen.get(a.sem.num, 0) < a.value:
                        seen[a.sem.num] = a.value
                        e.wait_ge(a.sem, a.value)
                last = o.run(e)
                if o.waited:
                    last.then_inc(o.sem, o.step)
        return body

    with nc.Block() as block:
        block.sync(program("sp"))
        block.gpsimd(program("pool"))
        block.scalar(program("act"))
        block.vector(program("dve"))
        block.tensor(program("pe"))
    nc.all_engine_barrier()
    nums = sorted(s.num for s in sems)
    assert nums == list(range(nums[0], nums[0] + len(nums)))
    nc.sync.sem_clear(range(nums[0], nums[-1] + 1))
    nc.all_engine_barrier()


def bcast(ap, shape):
    return ap.to_broadcast(shape)


def build(nc, a, out):
    with ExitStack() as ctx:
        def sb(name, shape, dt=F32):
            return ctx.enter_context(nc.sbuf_tensor(name, shape, dt))

        def sem(name):
            return ctx.enter_context(nc.semaphore(name))

        engines = ("pe", "act", "dve", "pool", "sp")
        f_sems = {e: sem(f"front_{e}") for e in engines}
        b_sems = {e: sem(f"back_{e}") for e in engines}
        s_x = sem("x_loaded")
        s_w = sem("weights_loaded")
        s_out = sem("out_stored")
        s_vs = [sem(f"v_shifted_{n}") for n in range(DEPTH * 2)]
        round_sems = [*f_sems.values(), *b_sems.values(), s_x, s_w, s_out, *s_vs]

        mb = [Bank(ctx.enter_context(nc.psum_tensor(f"f_bank{n}", [P, T], F32))) for n in range(4)]
        lb = [Bank(ctx.enter_context(nc.psum_tensor(f"b_bank{n}", [P, T], F32))) for n in range(4)]

        ident = sb("ident", [P, P])
        identb = sb("identb", [P, P], BF16)
        shift = sb("shift", [P, 2, P])
        selb = sb("selb", [96, 2 * NS], BF16)
        maskb = sb("maskb", [P, NT * P], BF16)
        half = sb("half", [P, NT])
        w_in = sb("w_in", [P, 2 * DI])
        conv_w = sb("conv_w", [P, NH2, NCONV])
        conv_b = sb("conv_b", [P, NH2])
        w_x = sb("w_x", [P, NH2, RANK + 2 * NS])
        w_dt = sb("w_dt", [2 * NS + RANK, DI])
        dt_b = sb("dt_b", [P, NH2])
        a_neg = sb("a_neg", [P, NH2, NS])
        d_par = sb("d_par", [P, NH2])
        w_out = sb("w_out", [P, NH2, D])
        wqkv = sb("wqkv", [P, DEPTH, 3 * INNER])
        wo = sb("wo", [P, DEPTH, NC, D])
        ln_g = sb("ln_g", [P, DEPTH])
        ln_b = sb("ln_b", [P, DEPTH])
        w1 = sb("w1", [P, DEPTH, 2 * HID])
        b1 = sb("b1", [P, DEPTH, 6])
        w2 = sb("w2", [P, DEPTH, 3, D])
        tab = sb("tab", [P, DEPTH, 4, NT, DH])
        scl = sb("scl", [P, DEPTH, 4, DH])

        x_in = sb("x_in", [P, NT, D])
        x_pad = sb("x_pad", [P, NH2, NCONV - 1 + T])
        u = sb("u", [P, NH2, T])
        zs = sb("zs", [P, NH2, T])
        bc3 = sb("bc3", [96, T], BF16)
        dt = sb("dt", [P, NH2, T])
        du = sb("du", [P, NH2, T])
        da = sb("da", [P, 2, NH2, T])
        dbu = sb("dbu", [P, NH2, T])
        hs = sb("hs", [P, 2, NH2, T])
        cs = sb("cs", [P, 2, T])
        gy = sb("gy", [P, 2, NH2, T])
        m_xn = gy[:, 0, 0, :].rearrange("p (t d) -> p t d", t=NT)
        bc_mid = gy[0:32, 1, 0, 0:T // 2].bitcast(BF16)
        xn_t = cs[:, 0, :]
        bc_r1 = cs[0:32, 1, :]
        dt_r = da[0:2 * NS + RANK, 0, 0, :]
        cv = hs[:, 0, :, :]
        dt_abs = hs[:, 1, :, :]
        yg = hs[:, 0, :, :]
        x1_next = sb("x1_next", [P, NT, D])
        x2_next = sb("x2_next", [P, NT, D])

        class Set:
            def __init__(self, banks, n, qr, kr, q_t, sq, m1, m2):
                self.banks = banks
                self.stat = sb(f"stat{n}", [P, NT, 6])
                self.mv = sb(f"mv{n}", [P, NT, 2])
                self.ve = sb(f"ve{n}", [P, NT])
                self.rs = sb(f"rs{n}", [P, NT])
                self.h_t = sb(f"h_t{n}", [P, T])
                self.sq, self.m1, self.m2, self.qr, self.kr, self.q_t = sq, m1, m2, qr, kr, q_t
                self.ss = sb(f"ss{n}", [P, NT, 2, HEADS])
                self.rn = sb(f"rn{n}", [P, NT, 2, HEADS])
                self.rn_t = sb(f"rn_t{n}", [P, NT, 2, HEADS])
                self.rq8 = sb(f"rq8{n}", [P, NT, HEADS])
                self.v = sb(f"v{n}", [P, NT, HEADS, DH + 1])
                self.vs = sb(f"vs{n}", [P, NT, HEADS, DH + 1])
                self.k_t = sb(f"k_t{n}", [P, NC, WIN + T])
                self.mx = sb(f"mx{n}", [P, HEADS, NT])
                self.nb = sb(f"nb{n}", [P, HEADS, NT])
                self.rd = sb(f"rd{n}", [P, HEADS, NT])
                self.pr = m1[:, :, :].rearrange("p b (t k) -> p b t k", t=NT)
                self.p_t, self.o, self.o_t = m2, qr, q_t

        flat2 = lambda x: x[:, :, :, :].rearrange("p a b n -> p (a b) n")
        a_log = x_pad[:, :, NCONV:NCONV + NS]
        front_set = Set(mb, 0, qr=flat2(da), kr=flat2(hs), q_t=flat2(gy), sq=dbu, m1=du, m2=dt)
        big = {n: sb(n, [P, NC, T]) for n in ("qr1", "kr1", "q_t1")}
        mid = {n: sb(n, [P, 2, T]) for n in ("sq1", "m11", "m21")}
        back_set = Set(lb, 1, qr=big["qr1"], kr=big["kr1"], q_t=big["q_t1"], sq=mid["sq1"], m1=mid["m11"],
                       m2=mid["m21"])
        rot = big["q_t1"][:, 0:2, :].rearrange("p c (a t d) -> p (c a) t d", a=2, t=NT)

        x_cur = sb("x_cur", [P, NT, D])
        xa = sb("xa", [P, NT, D])
        h2 = sb("h2", [P, NT, D])
        h2_t = big["qr1"][:, 0, :]
        ge = big["kr1"][:, 0:2, :]
        ff = sb("ff", [P, 3, T])
        o_buf = h2

        def load(s):
            loads = [
                (ident[:, :], a["c_ident"]),
                (shift[:, :, :], a["c_shift"].rearrange("a p n -> p a n")),
                (cs[:, 0, :], a["c_mask"]),
                (cs[0:96, 1, 0:2 * NS], a["c_sel"]),
                (w_in[:, :], a["L0_attn_in_proj_w"]),
                (w_x[:, :, 0:2 * NS], a["L0_attn_x_proj_w"][:, RANK:].rearrange("(h p) n -> p h n", p=P)),
                (w_x[:, :, 2 * NS:], a["L0_attn_x_proj_w"][:, 0:RANK].rearrange("(h p) n -> p h n", p=P)),
                (w_dt[2 * NS:, :], a["L0_attn_dt_proj_w"]),
                (w_out[:, :, :], a["L0_attn_out_proj_w"].rearrange("(h p) n -> p h n", p=P)),
                (conv_w[:, :, :], a["L0_attn_conv_w"].rearrange("(h p) k -> p h k", p=P)),
                (a_log[:, :, :], a["L0_attn_A_log"].rearrange("(h p) k -> p h k", p=P)),
                (wqkv[:, :, :], a["L0_ffn_wqkv"].rearrange("l p n -> p l n")),
                (w1[:, :, :], a["L0_ffn_w1"].rearrange("l p n -> p l n")),
                *((rot[:, q, :, :], a["c_rot"][q, :, :].rearrange("(t p) d -> p t d", p=P)) for q in range(4)),
            ]
            for dst, name in ((conv_b, "L0_attn_conv_b"), (dt_b, "L0_attn_dt_proj_b"), (d_par, "L0_attn_D_param")):
                loads.append((dst[:, :], a[name].rearrange("(h p) -> p h", p=P)))
            for dst, name in ((ln_g, "L0_ffn_ln_g"), (ln_b, "L0_ffn_ln_b")):
                loads.append((dst[:, :], a[name].rearrange("l p -> p l")))
            for l in range(DEPTH):
                loads.append((wo[:, l, :, :], a["L0_ffn_wo"][l, :, :].rearrange("(c p) n -> p c n", p=P)))
                for c, (c0, n) in enumerate(HCH):
                    loads.append((w2[0:n, l, c, :], a["L0_ffn_w2"][l, c0:c0 + n, :]))
                    for g in range(2):
                        src = a["L0_ffn_b1"][l:l + 1, g * HID + c0:g * HID + c0 + n]
                        loads.append((b1[0:n, l, 3 * g + c:3 * g + c + 1], src.rearrange("a p -> p a")))
                loads.append((w2[n:n + 1, l, 2, :], a["L0_ffn_b2"][l:l + 1, :]))
                for q, name in ((0, "L0_ffn_q_scale"), (2, "L0_ffn_k_scale")):
                    src = a[name][l:l + 1, :]
                    hd = DH // 2
                    for dst, piece in ((scl[:, l, q, :], src), (scl[:, l, q + 1, 0:hd], src[:, hd:DH]),
                                       (scl[:, l, q + 1, hd:DH], src[:, 0:hd])):
                        loads.append((dst, piece.to_broadcast([P, piece.shape[1]])))
            for n, (dst, src) in enumerate(loads):
                w = s.sp(lambda e, d=dst, r=src: e.dma_start(d, r, allow_slow_non_contiguous=True), s_w)
            s.dve(lambda e: e.memset(half[:, :], -0.5))
            s.dve(lambda e: e.memset(x_pad[:, :, 0:NCONV - 1], 0.0))
            for w_ in (front_set, back_set):
                s.dve(lambda e, w_=w_: e.memset(w_.h_t[DH:, 0:1], 0.0))
                s.dve(lambda e, w_=w_: e.memset(w_.k_t[:, :, 0:WIN], 0.0))
                s.dve(lambda e, w_=w_: e.memset(w_.v[:, :, :, :], 1.0))
                s.dve(lambda e, w_=w_: e.memset(w_.vs[0:WIN, 0, :, :], 0.0))
            s.dve(lambda e: e.memset(ff[:, 2, :], 1.0))
            s.dve(lambda e: e.tensor_copy(identb[:, :], ident[:, :]), w)
            s.dve(lambda e: e.tensor_copy(maskb[:, :], cs[:, 0, :]), w)
            s.dve(lambda e: e.tensor_copy(selb[:, :], cs[0:96, 1, 0:2 * NS]), w)
            for l in range(DEPTH):
                for q in range(4):
                    s.dve(lambda e, l=l, q=q: e.tensor_tensor(
                        tab[:, l, q, :, :], rot[:, q, :, :], bcast(scl[:, l, q:q + 1, :], [P, NT, DH]), ALU.mult), w)
            ex = s.act(lambda e: e.activation(a_neg[:, :, :], a_log[:, :, :], ACT.Exp), w)
            s.dve(lambda e: e.tensor_scalar(a_neg[:, :, :], a_neg[:, :, :], -1.0, None, ALU.mult), ex)

        def norm_scale(s, w, src, *after):
            for t in range(NT):
                n = s.dve(lambda e, t=t: e.bn_stats(w.stat[:, t, :], src(t)), *after, cost=0.2)
            for t in range(NT):
                n2 = s.dve(lambda e, t=t: e.bn_aggr(w.mv[:, t, :], w.stat[:, t, :]), n, cost=0.08)
            n3 = s.dve(lambda e: e.tensor_scalar(w.ve[:, :], w.mv[:, :, 1], EPS, None, ALU.add), n2, cost=0.07)
            return s.pool(lambda e: e.tensor_tensor(w.rs[:, :], w.ve[:, :], half[:, :], ALU.pow), n3, cost=0.96)

        def normalise(s, w, dst, src, *after):
            for t in range(NT):
                n = s.dve(lambda e, t=t: e.tensor_scalar(dst(t), src(t), w.mv[:, t, 0:1], w.rs[:, t:t + 1],
                                                         ALU.subtract, ALU.mult), *after, cost=0.26)
            return n

        def tm(bank):
            return bank.t[:, :].rearrange("p (t d) -> p t d", t=NT)

        def transposes(s, bank, src, *after):
            for n in range(4):
                last = s.pe(lambda e, n=n: e.transpose(bank.t[:, n * P:(n + 1) * P], src(n), ident[:, :]),
                            *after, *bank.readers, cost=0.11)
            return last

        def mamba(s, b, x1_free):
            w = front_set
            B0, B1, B2, B3 = mb
            ld = s.sp(lambda e: e.dma_start(x_in[:, :, :], a["L0_attn_x"][bass.ds(b, 1), :, :].rearrange(
                "b (t p) d -> p (b t) d", p=P)), s_x)
            rs = norm_scale(s, w, lambda t: x_in[:, t, :], ld)
            xn = normalise(s, w, lambda t: m_xn[:, t, :], lambda t: x_in[:, t, :], rs)
            tr = transposes(s, B0, lambda n: m_xn[:, n, :], xn)
            xt = s.act(lambda e: e.activation(xn_t, B0.t[:, :], ACT.Copy), tr)
            B0.readers = [xt]
            proj = []
            for c, bank in enumerate((B1, B2, B3, B0)):
                proj.append(s.pe(lambda e, c=c, bank=bank: e.matmul(
                    bank.t[:, :], w_in[:, c * P:(c + 1) * P], xn_t, start=True, stop=True),
                    xt, *bank.readers, cost=0.85))
            cv_done = []
            for h, bank in enumerate((B1, B2)):
                cp = s.act(lambda e, h=h, bank=bank: e.activation(
                    x_pad[:, h, NCONV - 1:], bank.t[:, :], ACT.Copy), proj[h])
                bank.readers = [cp]
                n = s.dve(lambda e, h=h: e.tensor_scalar(
                    cv[:, h, :], x_pad[:, h, NCONV - 1:], conv_w[:, h, NCONV - 1:NCONV], conv_b[:, h:h + 1],
                    ALU.mult, ALU.add), cp)
                for k in range(NCONV - 1):
                    n = s.dve(lambda e, h=h, k=k: e.scalar_tensor_tensor(
                        cv[:, h, :], x_pad[:, h, k:k + T], conv_w[:, h, k:k + 1], cv[:, h, :],
                        ALU.mult, ALU.add), n)
                cv_done.append(n)
            for h, bank in enumerate((B3, B0)):
                bank.readers = [s.act(lambda e, h=h, bank=bank: e.activation(zs[:, h, :], bank.t[:, :], ACT.Silu),
                                      proj[2 + h])]
            for h in range(NH2):
                us = s.act(lambda e, h=h: e.activation(u[:, h, :], cv[:, h, :], ACT.Silu), cv_done[h])
            for h in range(NH2):
                xp = s.pe(lambda e, h=h: e.matmul(B1.t[0:2 * NS + RANK, :], w_x[:, h, :], u[:, h, :],
                                                  start=h == 0, stop=h == 1), us, *B1.readers, cost=0.85)
            hi = s.act(lambda e: e.activation(bc3[0:32, :], B1.t[0:32, :], ACT.Copy), xp)
            dr = s.act(lambda e: e.activation(dt_r[32:40, :], B1.t[32:40, :], ACT.Copy), xp)
            r1 = s.dve(lambda e: e.tensor_tensor(bc_r1, B1.t[0:32, :], bc3[0:32, :], ALU.subtract),
                       hi, dr)
            B1.readers = [r1]
            mid = s.dve(lambda e: e.tensor_copy(bc_mid, bc_r1), r1)
            mid3 = s.act(lambda e: e.activation(bc3[32:64, :], bc_r1, ACT.Copy), r1)
            lo = s.dve(lambda e: e.tensor_tensor(bc3[64:96, :], bc_r1, bc_mid, ALU.subtract), mid)
            dts = []
            for h, bank in enumerate((B2, B3)):
                dp = s.pe(lambda e, h=h, bank=bank: e.matmul(
                    bank.t[:, :], w_dt[32:40, h * P:(h + 1) * P], dt_r[32:40, :], start=True, stop=True),
                    dr, *bank.readers, cost=0.85)
                ab = s.act(lambda e, h=h, bank=bank: e.activation(
                    dt_abs[:, h, :], bank.t[:, :], ACT.Abs, bias=dt_b[:, h:h + 1]), dp)
                rl = s.dve(lambda e, h=h, bank=bank: e.tensor_scalar(
                    dt[:, h, :], bank.t[:, :], dt_b[:, h:h + 1], 0.0, ALU.add, ALU.max), ab)
                bank.readers = [rl]
                dts.append((ab, rl))
            exs = [s.act(lambda e, h=h: e.activation(dt_abs[:, h, :], dt_abs[:, h, :], ACT.Exp, scale=-1.0), dts[h][0])
                   for h in range(NH2)]
            lns = [s.act(lambda e, h=h: e.activation(dt_abs[:, h, :], dt_abs[:, h, :], ACT.Ln, bias=1.0), exs[h])
                   for h in range(NH2)]
            for h in range(NH2):
                dd = s.dve(lambda e, h=h: e.tensor_tensor(dt[:, h, :], dt[:, h, :], dt_abs[:, h, :], ALU.add),
                           lns[h], dts[h][1])
                dudone = s.dve(lambda e, h=h: e.tensor_tensor(du[:, h, :], dt[:, h, :], u[:, h, :], ALU.mult), dd)
            acc = (B0, B1)
            das, scans, gs, ys = {}, {}, {}, {}

            def sum_state(n):
                for h in range(NH2):
                    ys[n, h] = s.pe(lambda e, h=h: e.matmul(
                        acc[h].t[:, :], ident[:, :], gy[:, n % 2, h, :], start=n == 0, stop=n == NS - 1),
                        gs[n, h], *(acc[h].readers if n == 0 else []), cost=0.85)

            cscp = {}
            for n in range(NS):
                j = n % 2
                bb = s.pe(lambda e, n=n: e.matmul(B2.t[:, :], selb[:, n:n + 1].to_broadcast([96, P]), bc3[:, :], start=True, stop=True),
                          hi, mid3, lo, *B2.readers, cost=0.22)
                cc = s.pe(lambda e, n=n: e.matmul(B3.t[:, :], selb[:, NS + n:NS + n + 1].to_broadcast([96, P]), bc3[:, :], start=True, stop=True),
                          *B3.readers, cost=0.22)
                for h in range(NH2):
                    das[n, h] = s.act(lambda e, n=n, h=h, j=j: e.activation(
                        da[:, j, h, :], dt[:, h, :], ACT.Exp, scale=a_neg[:, h, n:n + 1]),
                        dd, scans.get((n - 2, h)))
                cscp[n] = s.act(lambda e, j=j: e.activation(cs[:, j, :], B3.t[:, :], ACT.Copy),
                                cc, gs.get((n - 2, 1)))
                B3.readers = [cscp[n]]
                for h in range(NH2):
                    db = s.dve(lambda e, h=h: e.tensor_tensor(dbu[:, h, :], du[:, h, :], B2.t[:, :], ALU.mult),
                               bb, dudone)
                    scans[n, h] = s.dve(lambda e, h=h, j=j: e.tensor_tensor_scan(
                        hs[:, j, h, :], da[:, j, h, :], dbu[:, h, :], 0.0, ALU.mult, ALU.add),
                        db, das[n, h], gs.get((n - 2, h)))
                B2.readers = [db]
                for h in range(NH2):
                    gs[n, h] = s.pool(lambda e, h=h, j=j: e.tensor_tensor(
                        gy[:, j, h, :], hs[:, j, h, :], cs[:, j, :], ALU.mult),
                        scans[n, h], cscp[n], ys.get((n - 2, h)), cost=1.2)
                if n:
                    sum_state(n - 1)
            sum_state(NS - 1)
            for h in range(NH2):
                yd = s.dve(lambda e, h=h: e.scalar_tensor_tensor(
                    yg[:, h, :], u[:, h, :], d_par[:, h:h + 1], acc[h].t[:, :], ALU.mult, ALU.add), ys[NS - 1, h])
                acc[h].readers = [yd]
                yz = s.dve(lambda e, h=h: e.tensor_tensor(yg[:, h, :], yg[:, h, :], zs[:, h, :], ALU.mult), yd)
            for t in range(NT):
                for h in range(NH2):
                    op = s.pe(lambda e, t=t, h=h: e.matmul(
                        B2.t[:, t * P:(t + 1) * P], yg[:, h, t * P:(t + 1) * P], w_out[:, h, :],
                        start=h == 0, stop=h == 1), yz, *B2.readers, cost=0.21)
            rs = norm_scale(s, w, lambda t: B2.t[:, t * P:(t + 1) * P], op)
            xn = normalise(s, w, lambda t: m_xn[:, t, :], lambda t: B2.t[:, t * P:(t + 1) * P], rs)
            B2.readers = [xn]
            return s.dve(lambda e: e.tensor_tensor(x1_next[:, :, :], m_xn[:, :, :], x_in[:, :, :], ALU.add),
                         xn, x1_free)

        def front(s, b, x1_free, x2_free):
            for k in mb:
                k.readers = []
            x1 = mamba(s, b, x1_free)
            w = front_set
            rs = norm_scale(s, w, lambda t: x1_next[:, t, :], x1)
            xn = normalise(s, w, lambda t: x2_next[:, t, :], lambda t: x1_next[:, t, :], rs, x2_free)
            attention(s, w, 0, x2_next, xn)

        def back(s, b):
            for k in lb:
                k.readers = []
            w = back_set
            c1 = s.dve(lambda e: e.tensor_copy(x_cur[:, :, :], x1_next[:, :, :]), cost=0.34)
            c2 = s.dve(lambda e: e.tensor_copy(xa[:, :, :], x2_next[:, :, :]), cost=0.34)
            x = feed_forward(s, w, 0, c2)
            x = feed_forward(s, w, 1, attention(s, w, 1, xa, x))
            rs = norm_scale(s, w, lambda t: xa[:, t, :], x)
            xn = normalise(s, w, lambda t: xa[:, t, :], lambda t: xa[:, t, :], rs)
            wr = s.dve(lambda e: e.tensor_tensor(o_buf[:, :, :], xa[:, :, :], x_cur[:, :, :], ALU.add), xn)
            store = s.sp(lambda e: e.dma_start(out[bass.ds(b, 1), :, :].rearrange(
                "b (t p) d -> p (b t) d", p=P), o_buf[:, :, :]), s_out, wr)
            s.add("sp", lambda e: None, store)
            return c1, c2

        def attention(s, w, l, x, x_done):
            L0, L1, L2, L3 = w.banks
            h_t, sq, m1, m2, qr, kr, q_t, k_t, v, vs = (w.h_t, w.sq, w.m1, w.m2, w.qr, w.kr, w.q_t, w.k_t, w.v, w.vs)
            ss, rn, rn_t, rq8, mx, nb, rd, pr, p_t, o, o_t = (w.ss, w.rn, w.rn_t, w.rq8, w.mx, w.nb, w.rd, w.pr,
                                                              w.p_t, w.o, w.o_t)
            tr = transposes(s, L0, lambda n: x[:, n, :], x_done)
            c0 = s.act(lambda e: e.activation(h_t[0:DH, :], L0.t[0:DH, :], ACT.Copy), tr)
            c1 = s.act(lambda e: e.activation(h_t[DH:, 1:T], L0.t[DH:, 0:T - 1], ACT.Copy), tr)
            L0.readers = [c1]
            ring, at = [L1, L2, L3, L0], 0
            sq_read, m_read, added = {}, {}, {}
            qt, kt = {}, {}
            heads = lambda x: x.rearrange("p (h d) -> p h d", h=HEADS)
            halves = lambda x: x.rearrange("p (h a d) -> p h a d", h=HEADS, a=2)

            def bank_of():
                nonlocal at
                at += 1
                return ring[(at - 1) % 4]

            def project(t, part):
                bank = bank_of()
                mm = s.pe(lambda e: e.matmul(
                    bank.t[:, :], h_t[:, t * P:(t + 1) * P], wqkv[:, l, part * INNER:(part + 1) * INNER],
                    start=True, stop=True), c0, c1, *bank.readers)
                return bank, mm

            def rotate(t, part):
                bank, mm = project(t, part)
                sqd = s.act(lambda e: e.activation(sq[:, part, :], bank.t[:, :], ACT.Square), mm, sq_read.get(part))
                sq_read[part] = s.dve(lambda e: e.tensor_reduce(
                    ss[:, t, part, :], heads(sq[:, part, :]), AX, ALU.add), sqd)
                table = [bcast(tab[:, l, 2 * part + n, t:t + 1, :], [P, HEADS, DH]).rearrange(
                    "p h (a d) -> p h a d", a=2) for n in range(2)]
                s.dve(lambda e: e.tensor_tensor(halves(m1[:, part, :]), halves(bank.t[:, :]), table[0], ALU.mult),
                      sqd, m_read.get(part))
                mc = s.dve(lambda e: e.tensor_tensor(halves(m2[:, part, :]), halves(bank.t[:, :])[:, :, ::-1, :],
                                                     table[1], ALU.mult), sqd)
                bank.readers = [mc]
                m_read[part] = added[t, part] = s.pool(lambda e: e.tensor_tensor(
                    (qr, kr)[part][:, t, :], m1[:, part, :], m2[:, part, :], ALU.add), mc)

            def value(t):
                bank, mm = project(t, 2)
                vc = s.act(lambda e: e.activation(v[:, t, :, 0:DH], heads(bank.t[:, :]), ACT.Copy), mm)
                bank.readers = [vc]
                return vc

            def inverse_norms(t0, t1):
                flat = lambda x: x[:, t0:t1, :, :].rearrange("p t a h -> p (t a h)")
                n = s.dve(lambda e: e.tensor_scalar(flat(ss), flat(ss), 1e-24, None, ALU.max), *sq_read.values(),
                          cost=0.1)
                n = s.dve(lambda e: e.tensor_single_scalar(flat(rn_t).bitcast(I32), flat(ss).bitcast(I32), 1,
                                                           ALU.arith_shift_right), n, cost=0.1)
                n = s.dve(lambda e: e.tensor_scalar(flat(rn).bitcast(I32), flat(rn_t).bitcast(I32), -1.0,
                                                    float(MAGIC), ALU.mult, ALU.add), n, cost=0.1)
                for _ in range(3):
                    n = s.dve(lambda e: e.scalar_tensor_tensor(flat(rn_t), flat(ss), -0.5, flat(rn),
                                                               ALU.mult, ALU.mult), n, cost=0.1)
                    n = s.dve(lambda e: e.tensor_tensor(flat(rn_t), flat(rn_t), flat(rn), ALU.mult), n, cost=0.1)
                    n = s.dve(lambda e: e.scalar_tensor_tensor(flat(rn), flat(rn_t), 1.5, flat(rn),
                                                               ALU.add, ALU.mult), n, cost=0.1)
                return n, s.dve(lambda e: e.tensor_scalar(rq8[:, t0:t1, :], rn[:, t0:t1, 0, :], 8.0, None, ALU.mult),
                                n, cost=0.1)

            def channel_major(t, dst, off, src, *after):
                bank = bank_of()
                tr = transposes(s, bank, lambda c: src[:, t, c * P:(c + 1) * P], *after)
                cp = s.act(lambda e: e.activation(dst[:, :, off + t * P:off + (t + 1) * P], bank.t[:, :].rearrange(
                    "p (c n) -> p c n", c=NC), ACT.Copy), tr)
                bank.readers = [cp]
                return cp

            def keys(t, n):
                kn = s.dve(lambda e: e.tensor_tensor(
                    heads(kr[:, t, :]), heads(kr[:, t, :]), bcast(rn[:, t, 1, :].unsqueeze(2), [P, HEADS, DH]),
                    ALU.mult), n, added[t, 1])
                return channel_major(t, k_t, WIN, kr, kn)

            rotate(0, 1), rotate(0, 0), value(0)
            rotate(1, 1), rotate(1, 0)
            channel_major(0, q_t, 0, qr, added[0, 0])
            value(1)
            n01, _ = inverse_norms(0, 2)
            rotate(2, 1)
            channel_major(1, q_t, 0, qr, added[1, 0])
            rotate(2, 0)
            value(2)
            keys(0, n01)
            rotate(3, 1)
            channel_major(2, q_t, 0, qr, added[2, 0])
            rotate(3, 0)
            vc = value(3)
            keys(1, n01)
            n23, q8 = inverse_norms(2, 4)
            channel_major(3, q_t, 0, qr, added[3, 0])
            keys(2, n23)
            qk = keys(3, n23)
            v1 = s.sp(lambda e: e.dma_start(vs[0:WIN, 1:NT, :, :], v[WIN:, 0:NT - 1, :, :]), s_vs[2 * l], vc)
            v2 = s.sp(lambda e: e.dma_start(vs[WIN:, :, :, :], v[0:WIN, :, :, :]), s_vs[2 * l + 1], vc)
            weights, pts, copies, avs = {}, {}, {}, {}
            ot = L3.t[:, 0:NT * (DH + 1)].rearrange("p (t d) -> p t d", t=NT)

            def scores(hd):
                c, r, bank = hd // 2, DH * (hd % 2), (L0, L1)[hd % 2]
                s.pe(lambda e: e.matmul(bank.t[:, :], identb[:, :], maskb[:, :], start=True, stop=False,
                                        skip_group_check=True), *bank.readers, cost=0.22)
                for p in range(NT):
                    for j in range(2):
                        last = s.pe(lambda e, p=p, j=j: e.matmul(
                            bank.t[WIN * j:WIN * j + WIN, p * P:(p + 1) * P],
                            q_t[r:r + DH, c, p * P + WIN * j:p * P + WIN * j + WIN],
                            k_t[r:r + DH, c, p * P + WIN * j:p * P + WIN * j + P],
                            start=False, stop=True, skip_group_check=True), qk, cost=0.12)
                return last

            def softmax(hd, sc):
                bank = (L0, L1)[hd % 2]
                m = s.dve(lambda e: e.tensor_reduce(
                    mx[:, hd, :], bank.t[:, :].rearrange("p (t k) -> p t k", t=NT), AX, ALU.max), sc)
                n = s.dve(lambda e: e.scalar_tensor_tensor(
                    nb[:, hd, :], mx[:, hd, :], -1.0, rq8[:, :, hd], ALU.mult, ALU.mult), m, q8, cost=0.08)
                for p in range(NT):
                    last = s.act(lambda e, p=p: e.activation(
                        pr[:, hd % 2, p, :], bank.t[:, p * P:(p + 1) * P], ACT.Exp, bias=nb[:, hd, p:p + 1],
                        scale=rq8[:, p, hd:hd + 1]), n, pts.get(hd - 2), cost=0.35)
                bank.readers = [last]
                return last

            def keys_in_partitions(hd):
                pts[hd] = transposes(s, L2, lambda n: pr[:, hd % 2, n, :], weights[hd])
                if hd % 4 != 3:
                    cp = s.dve(lambda e: e.tensor_copy(p_t[:, hd % 2, :], L2.t[:, :]), pts[hd], avs.get(hd - 2))
                else:
                    cp = s.act(lambda e: e.activation(p_t[:, hd % 2, :], L2.t[:, :], ACT.Copy), pts[hd],
                               avs.get(hd - 2))
                L2.readers = [cp]
                return cp

            def values(hd):
                for p in range(NT):
                    for j in range(2):
                        avs[hd] = s.pe(lambda e, p=p, j=j: e.matmul(
                            ot[WIN * j:WIN * j + WIN, p, :],
                            p_t[:, hd % 2, p * P + WIN * j:p * P + WIN * j + WIN],
                            (vs, v)[j][:, p, hd, :], start=True, stop=True),
                            copies[hd], v1, v2, *L3.readers, cost=0.09)
                rc = s.dve(lambda e: e.reciprocal(rd[:, hd, :], ot[:, :, DH]), avs[hd], cost=0.09)
                od = s.dve(lambda e: e.tensor_tensor(
                    o[:, :, hd * DH:(hd + 1) * DH], ot[:, :, 0:DH],
                    bcast(rd[:, hd, :].unsqueeze(2), [P, NT, DH]), ALU.mult), rc, cost=0.33)
                L3.readers = [od]
                return od

            for i in range(HEADS + 2):
                if i < HEADS:
                    weights[i] = softmax(i, scores(i))
                if 0 < i <= HEADS:
                    copies[i - 1] = keys_in_partitions(i - 1)
                if i > 1:
                    od = values(i - 2)
            oc = {}
            for c in range(NC):
                bank = (L0, L1, L2, L0)[c]
                tr = transposes(s, bank, lambda n, c=c: o[:, n, c * P:(c + 1) * P], od)
                oc[c] = s.act(lambda e, c=c, bank=bank: e.activation(o_t[:, c, :], bank.t[:, :], ACT.Copy), tr)
                bank.readers = [oc[c]]
            for t in range(NT):
                for c in range(NC):
                    mm = s.pe(lambda e, t=t, c=c: e.matmul(
                        L3.t[:, t * P:(t + 1) * P], o_t[:, c, t * P:(t + 1) * P], wo[:, l, c, :],
                        start=c == 0, stop=c == NC - 1), oc[c], *L3.readers, cost=0.21)
            x2 = s.dve(lambda e: e.tensor_tensor(x[:, :, :], x[:, :, :], tm(L3), ALU.add), mm)
            L3.readers = [x2]
            return x2

        def feed_forward(s, w, l, x2):
            L0, L1, L2, L3 = w.banks
            sh = L0.t[:, 0:NT * DH].rearrange("p (t d) -> p t d", t=NT)
            s.pe(lambda e: e.matmul(sh, shift[:, 0, :], xa[:, :, DH:], start=True, stop=False,
                                    skip_group_check=True), x2, *L0.readers, cost=0.43)
            mm = s.pe(lambda e: e.matmul(sh[:, 1:, :], shift[:, 1, :], xa[:, 0:NT - 1, DH:], start=False, stop=True,
                                         skip_group_check=True), cost=0.32)
            ha = s.pool(lambda e: e.tensor_copy(h2[:, :, 0:DH], xa[:, :, 0:DH]), x2)
            hb = s.act(lambda e: e.activation(h2[:, :, DH:], sh, ACT.Copy), mm, cost=0.35)
            L0.readers = [hb]
            rs = norm_scale(s, w, lambda t: h2[:, t, :], ha, hb)
            hn = normalise(s, w, lambda t: h2[:, t, :], lambda t: h2[:, t, :], rs)
            tr = transposes(s, L1, lambda n: h2[:, n, :], hn)
            ht = s.act(lambda e: e.activation(h2_t, L1.t[:, :], ACT.Identity, bias=ln_b[:, l:l + 1],
                                              scale=ln_g[:, l:l + 1]), tr)
            L1.readers = [ht]
            ge_read = {}
            for c, (c0_, n) in enumerate(HCH):
                ab, gb = ((L2, L3), (L0, L1), (L2, L3))[c]
                mg = s.pe(lambda e, c0_=c0_, n=n, gb=gb: e.matmul(
                    gb.t[0:n, :], w1[:, l, HID + c0_:HID + c0_ + n], h2_t, start=True, stop=True),
                    ht, *gb.readers, cost=0.85)
                ma = s.pe(lambda e, c0_=c0_, n=n, ab=ab: e.matmul(
                    ab.t[0:n, :], w1[:, l, c0_:c0_ + n], h2_t, start=True, stop=True),
                    ht, *ab.readers, cost=0.85)
                gd = s.act(lambda e, c=c, n=n, gb=gb: e.activation(
                    ge[0:n, c % 2, :], gb.t[0:n, :], ACT.Gelu, bias=b1[0:n, l, 3 + c:4 + c]), mg, ge_read.get(c % 2))
                gb.readers = [gd]
                ge_read[c % 2] = fd = s.dve(lambda e, c=c, n=n, ab=ab: e.scalar_tensor_tensor(
                    ff[0:n, c, :], ab.t[0:n, :], b1[0:n, l, c:c + 1], ge[0:n, c % 2, :], ALU.add, ALU.mult), ma, gd)
                ab.readers = [fd]
            for t in range(NT):
                for c, (c0_, n) in enumerate(HCH):
                    k = n + (c == 2)
                    mm = s.pe(lambda e, t=t, c=c, k=k: e.matmul(
                        L0.t[:, t * P:(t + 1) * P], ff[0:k, c, t * P:(t + 1) * P], w2[0:k, l, c, :],
                        start=c == 0, stop=c == 2), fd, *L0.readers, cost=0.21)
            x3 = s.dve(lambda e: e.tensor_tensor(xa[:, :, :], xa[:, :, :], tm(L0), ALU.add), mm)
            L0.readers = [x3]
            return x3

        s = Stage(f_sems)
        load(s)
        run_block(nc, s.ops, round_sems)

        s = Stage(f_sems)
        front(s, 0, None, None)
        run_block(nc, s.ops, round_sems)

        with nc.Fori(0, B - 1) as i:
            sl, sm = Stage(b_sems), Stage(f_sems)
            x1_copied, x2_copied = back(sl, i)
            front(sm, i + 1, x1_copied, x2_copied)
            run_block(nc, merged([sl, sm]), round_sems)

        s = Stage(b_sems)
        back(s, B - 1)
        run_block(nc, s.ops, round_sems)

_INS = ["L0_attn_x", "L0_attn_in_proj_w", "L0_attn_conv_w", "L0_attn_conv_b", "L0_attn_x_proj_w",
        "L0_attn_dt_proj_w", "L0_attn_dt_proj_b", "L0_attn_A_log", "L0_attn_D_param", "L0_attn_out_proj_w",
        "L0_ffn_wqkv", "L0_ffn_q_scale", "L0_ffn_k_scale", "L0_ffn_wo", "L0_ffn_ln_g", "L0_ffn_ln_b",
        "L0_ffn_w1", "L0_ffn_b1", "L0_ffn_w2", "L0_ffn_b2"]


def constants():
    f = np.float32
    c = {"c_ident": np.eye(P, dtype=f)}
    sh = np.zeros((2, P, P), f)
    sh[0, np.arange(P - 1), np.arange(1, P)] = 1
    sh[1, P - 1, 0] = 1
    c["c_shift"] = sh
    c["c_sel"] = np.tile(np.eye(2 * NS, dtype=f), (3, 1))
    q, k = np.arange(P)[:, None], np.arange(P)[None, :]
    i = q % WIN
    bad = (i + WIN < k) | (i + WIN > k + WIN)
    m = np.zeros((P, NT, P), bool)
    m[:] = bad[:, None, :]
    m[0:WIN, 0, 0:WIN] = True
    c["c_mask"] = np.where(m, f(NEG), f(0)).reshape(P, NT * P)
    hi = np.arange(0, DH, 2, dtype=f)
    inv = f(1) / f(10000.0) ** (hi / f(DH))
    t = np.arange(T, dtype=f)
    fr = np.concatenate([t[:, None] * inv[None, :]] * 2, -1)
    base = (hi + f(0.4 * DH)) / f(1.4 * DH)
    power = (t - T // 2) / f(WIN // 2)
    sc = np.concatenate([base[None, :] ** power[:, None]] * 2, -1)
    sign = np.where(np.arange(DH) < DH // 2, f(-1), f(1))
    cos, sin = np.cos(fr), np.sin(fr) * sign
    c["c_rot"] = np.stack([cos * sc, sin * sc, cos / sc, sin / sc]).astype(f)
    return c


def kernel(**inputs):
    import concourse.bacc as _bacc
    from concourse.bass_utils import run_bass_kernel_spmd as _run

    nc = _bacc.Bacc("TRN2", target_bir_lowering=False, num_devices=1)
    arrays, aps = {}, {}
    for name, x in [*((n, inputs[n]) for n in _INS), *constants().items()]:
        x = np.ascontiguousarray(x)
        arrays[f"in_{name}"] = x
        aps[name] = nc.dram_tensor(f"in_{name}", x.shape, mybir.dt.from_np(x.dtype), kind="ExternalInput").ap()
    out = nc.dram_tensor("out_dram", (B, T, D), F32, kind="ExternalOutput").ap()
    build(nc, aps, out)
    r = _run(nc, [arrays], core_ids=[0])
    return r.results[0]["out_dram"]
```

```python
from contextlib import ExitStack
from itertools import count, cycle

import numpy as np

import concourse.bass as bass
from concourse import mybir

F32 = mybir.dt.float32
BF16 = mybir.dt.bfloat16
I32 = mybir.dt.int32
ALU = mybir.AluOpType
ACT = mybir.ActivationFunctionType
AX = mybir.AxisListType.X

B, T, D = 16, 512, 128
P = 128
NT = T // P
DI, NH2 = 256, 2
NS, NCONV, RANK = 16, 4, 8
DEPTH, HEADS, DH, WIN = 2, 8, 64, 64
INNER = HEADS * DH
NC = INNER // P
HID = 341
HCH = [(0, 128), (128, 128), (256, HID - 256)]
EPS = 1e-5
NEG = -1.0e30
MAGIC = 0x5F3759DF


class Op:

    numbers = count()

    def __init__(self, engine, run, after, cost, sem, step, table=None):
        self.number = next(Op.numbers)
        self.table = table
        self.engine, self.run, self.cost, self.sem, self.step = engine, run, cost, sem, step
        self.after = [a for a in after if a is not None]
        self.value = None
        for a in self.after:
            a.waited = True
        self.waited = step == 16


class Stage:

    def __init__(self, sems):
        self.sems, self.ops = sems, []

    def add(self, engine, run, *after, cost=None, dma=None, table=None):
        cost = cost if cost is not None else {"pe": 0.85, "act": 0.48, "dve": 0.6, "pool": 1.22, "sp": 0.0}[engine]
        self.ops.append(Op(engine, run, after, cost, dma or self.sems[engine], 16 if dma else 1, table))
        return self.ops[-1]

    def pe(self, run, *after, **k):
        return self.add("pe", run, *after, **k)

    def act(self, run, *after, **k):
        return self.add("act", run, *after, **k)

    def dve(self, run, *after, **k):
        return self.add("dve", run, *after, **k)

    def pool(self, run, *after, **k):
        return self.add("pool", run, *after, **k)

    def sp(self, run, dma, *after, **k):
        return self.add("sp", run, *after, dma=dma, **k)


class Bank:

    def __init__(self, tile):
        self.t, self.readers = tile, []


LATENCY = {"pe": 0.2, "act": 0.25, "dve": 0.15, "pool": 0.2, "sp": 2.0}


TABLE_LOAD = 1.3
EXP_LN, GELU, SILU = "natural_log_exp_and_others", "gelu_and_others", "silu_and_others"


TABLE_LOAD = 1.3
EXP_LN, GELU, SILU = "natural_log_exp_and_others", "gelu_and_others", "silu_and_others"
HURRY = (0.05, 0.05, 0.4)


def to_the_end(ops):
    length, queue_next, followers = {}, {}, {}
    for o in sorted(ops, key=lambda o: -o.number):
        queue = (o.sem.num, o.engine)
        behind = [length[x] + LATENCY[o.engine] for x in followers.get(o, [])]
        if queue in queue_next:
            behind.append(length[queue_next[queue]])
        length[o] = o.cost + max(behind, default=0.0)
        queue_next[queue] = o
        for x in o.after:
            followers.setdefault(x, []).append(o)
    return length


def play(queues, before, gap, hurry, weight):
    heads = [dict.fromkeys(LATENCY, 0) for _ in queues]
    free, end, table = dict.fromkeys(LATENCY, 0.0), {}, None
    while True:
        best = None
        for n, q in enumerate(queues):
            for e in LATENCY:
                if heads[n][e] == len(q[e]):
                    continue
                o = q[e][heads[n][e]]
                if any(x not in end for x in before(o)):
                    continue
                load = TABLE_LOAD if o.table not in (None, table) else 0.0
                start = max([free[e] + load] + [end[x] + gap(x, o) for x in before(o)])
                key = (start - hurry * weight[o], n, e)
                if best is None or key < best[0]:
                    best = (key, o, start)
        if best is None:
            return end
        (_, n, e), o, start = best
        table = o.table or table
        heads[n][e] += 1
        free[e] = start + (0.05 if e == "sp" else o.cost)
        end[o] = start + o.cost


def merged(stages):
    ops = [o for s in stages for o in s.ops]
    followers = {o: [] for o in ops}
    for o in ops:
        for x in o.after:
            followers[x].append(o)
    queues = [{e: [o for o in s.ops if o.engine == e] for e in LATENCY} for s in stages]
    backwards = [{e: q[e][::-1] for e in LATENCY} for q in queues]
    forth = (lambda o: o.after), (lambda x, o: LATENCY[x.engine])
    back = (lambda o: followers[o]), (lambda x, o: LATENCY[o.engine])
    end = play(queues, *forth, HURRY[0], to_the_end(ops))
    left = play(backwards, *back, HURRY[1], end)
    end = play(queues, *forth, HURRY[2], left)
    assert len(end) == len(ops)
    return list(end)


def run_block(nc, ops, sems):
    count = {}
    for o in ops:
        if o.waited:
            count[o.sem.num] = count.get(o.sem.num, 0) + o.step
            o.value = count[o.sem.num]

    def program(name):
        def body(e):
            seen, table = {}, None
            for o in ops:
                if o.engine != name:
                    continue
                if o.table not in (None, table):
                    table = o.table
                    e.preload_act_table_set(table)
                for a in o.after:
                    if seen.get(a.sem.num, 0) < a.value:
                        seen[a.sem.num] = a.value
                        e.wait_ge(a.sem, a.value)
                last = o.run(e)
                if o.waited:
                    last.then_inc(o.sem, o.step)
        return body

    with nc.Block() as block:
        block.sync(program("sp"))
        block.gpsimd(program("pool"))
        block.scalar(program("act"))
        block.vector(program("dve"))
        block.tensor(program("pe"))
    nc.all_engine_barrier()
    nums = sorted(s.num for s in sems)
    assert nums == list(range(nums[0], nums[0] + len(nums)))
    nc.sync.sem_clear(range(nums[0], nums[-1] + 1))
    nc.all_engine_barrier()


def bcast(ap, shape):
    return ap.to_broadcast(shape)


def build(nc, a, out):
    with ExitStack() as ctx:
        def sb(name, shape, dt=F32):
            return ctx.enter_context(nc.sbuf_tensor(name, shape, dt))

        def sem(name):
            return ctx.enter_context(nc.semaphore(name))

        engines = ("pe", "act", "dve", "pool", "sp")
        f_sems = {e: sem(f"front_{e}") for e in engines}
        b_sems = {e: sem(f"back_{e}") for e in engines}
        e_sems = {e: sem(f"enter_{e}") for e in engines}
        s_x = sem("x_loaded")
        s_w = sem("enter_weights_loaded")
        s_w2 = sem("weights_loaded")
        t_sems = {e: sem(f"tables_{e}") for e in engines}
        s_out = sem("out_stored")
        s_vs = [sem(f"v_shifted_{n}") for n in range(DEPTH * 2)]
        block_sems = [*f_sems.values(), *b_sems.values(), *e_sems.values(), *t_sems.values(),
                      s_x, s_w, s_w2, s_out, *s_vs]

        mb = [Bank(ctx.enter_context(nc.psum_tensor(f"f_bank{n}", [P, T], F32))) for n in range(4)]
        lb = [Bank(ctx.enter_context(nc.psum_tensor(f"b_bank{n}", [P, T], F32))) for n in range(4)]

        ident = sb("ident", [P, P])
        identb = sb("identb", [P, P], BF16)
        shift = sb("shift", [P, 2, P])
        selb = sb("selb", [96, 2 * NS], BF16)
        maskb = sb("maskb", [P, NT * P], BF16)
        half = sb("half", [P, NT])
        w_in = sb("w_in", [P, 2 * DI])
        conv_w = sb("conv_w", [P, NH2, NCONV])
        conv_b = sb("conv_b", [P, NH2])
        w_x = sb("w_x", [P, NH2, RANK + 2 * NS])
        w_dt = sb("w_dt", [2 * NS + RANK, DI])
        dt_b = sb("dt_b", [P, NH2])
        a_neg = sb("a_neg", [P, NH2, NS])
        d_par = sb("d_par", [P, NH2])
        w_out = sb("w_out", [P, NH2, D])
        wqkv = sb("wqkv", [P, DEPTH, 3 * INNER])
        wo = sb("wo", [P, DEPTH, NC, D])
        ln_g = sb("ln_g", [P, DEPTH])
        ln_b = sb("ln_b", [P, DEPTH])
        w1 = sb("w1", [P, DEPTH, 2 * HID])
        b1 = sb("b1", [P, DEPTH, 6])
        w2 = sb("w2", [P, DEPTH, 3, D])
        tab = sb("tab", [P, DEPTH, 4, NT, DH])
        scl = sb("scl", [P, DEPTH, 4, DH])

        x_in = sb("x_in", [P, NT, D])
        u = sb("u", [P, NH2, T])
        zs = sb("zs", [P, NH2, T])
        bc3 = sb("bc3", [96, T], BF16)
        dt = sb("dt", [P, NH2, T])
        du = sb("du", [P, NH2, T])
        da = sb("da", [P, 2, NH2, T])
        dbu = sb("dbu", [P, NH2, T])
        hs = sb("hs", [P, 2, NH2, T])
        cs = sb("cs", [P, 2, T])
        gy = sb("gy", [P, 2, NH2, T])
        m_ln = gy[:, 0, 0, :].rearrange("p (t d) -> p t d", t=NT)
        yg = hs[:, 0, :, :]
        x1_next = sb("x1_next", [P, NT, D])
        x2_next = sb("x2_next", [P, NT, D])

        class Set:
            def __init__(self, banks, n, qr, kr, q_t, sq, m1, m2):
                self.banks = banks
                self.stat = sb(f"stat{n}", [P, NT, 6])
                self.mv = sb(f"mv{n}", [P, NT, 2])
                self.ve = sb(f"ve{n}", [P, NT])
                self.rs = sb(f"rs{n}", [P, NT])
                self.h_t = sb(f"h_t{n}", [P, T])
                self.sq, self.m1, self.m2, self.qr, self.kr, self.q_t = sq, m1, m2, qr, kr, q_t
                self.ss = sb(f"ss{n}", [P, 2, NT, HEADS])
                self.rn = sb(f"rn{n}", [P, 2, NT, HEADS])
                self.rn_t = sb(f"rn_t{n}", [P, 2, NT, HEADS])
                self.rq8 = sb(f"rq8{n}", [P, NT, HEADS])
                self.v = sb(f"v{n}", [P, NT, HEADS, DH + 1])
                self.vs = sb(f"vs{n}", [P, NT, HEADS, DH + 1])
                self.k_t = sb(f"k_t{n}", [P, NC, WIN + T])
                self.mx = sb(f"mx{n}", [P, HEADS, NT])
                self.nb = sb(f"nb{n}", [P, HEADS, NT])
                self.rd = sb(f"rd{n}", [P, HEADS, NT])
                self.pr = m1[:, :, :].rearrange("p b (t k) -> p b t k", t=NT)
                self.p_t, self.o, self.o_t = m2, qr, q_t

        flat2 = lambda x: x[:, :, :, :].rearrange("p a b n -> p (a b) n")
        front_set = Set(mb, 0, qr=flat2(da), kr=flat2(hs), q_t=flat2(gy), sq=dbu, m1=cs,
                        m2=sb("m20", [P, 2, T]))
        big = {n: sb(n, [P, NC, T]) for n in ("qr1", "kr1", "q_t1")}
        mid = {n: sb(n, [P, 2, T]) for n in ("sq1", "m11", "m21")}
        back_set = Set(lb, 1, qr=big["qr1"], kr=big["kr1"], q_t=big["q_t1"], sq=mid["sq1"], m1=mid["m11"],
                       m2=mid["m21"])
        rot = big["kr1"][:, 0:2, :].rearrange("p c (a t d) -> p (c a) t d", a=2, t=NT)

        q_flat = big["q_t1"][:, :, :].rearrange("p c n -> p (c n)")
        n_pad = NCONV - 1 + T
        x_pad = q_flat[:, 0:NH2 * n_pad].rearrange("p (h n) -> p h n", h=NH2)
        e_xn = q_flat[:, NH2 * n_pad:NH2 * n_pad + T].rearrange("p (t d) -> p t d", t=NT)
        xn_t = big["qr1"][:, 1, :]
        bc_r1 = big["qr1"][0:32, 2, :]
        dt_r = big["qr1"][0:2 * NS + RANK, 3, :]
        bc_mid = mid["sq1"][0:32, 0, 0:T // 2].bitcast(BF16)
        cv, dt_abs = mid["m11"], mid["m21"]
        e_stat = sb("e_stat", [P, NT, 6])
        e_mv = sb("e_mv", [P, NT, 2])
        e_ve = sb("e_ve", [P, NT])
        e_rs = sb("e_rs", [P, NT])
        a_log = big["kr1"][:, 2:4, 0:NS]

        x_cur = sb("x_cur", [P, NT, D])
        xa = sb("xa", [P, NT, D])
        h2 = sb("h2", [P, NT, D])
        h2_t = big["qr1"][:, 0, :]
        ge = big["kr1"][:, 0:2, :]
        ff = sb("ff", [P, 3, T])
        o_buf = h2

        def load(s):
            loads = [
                (ident[:, :], a["c_ident"]),
                (w_in[:, :], a["L0_attn_in_proj_w"]),
                (w_x[:, :, 0:2 * NS], a["L0_attn_x_proj_w"][:, RANK:].rearrange("(h p) n -> p h n", p=P)),
                (w_x[:, :, 2 * NS:], a["L0_attn_x_proj_w"][:, 0:RANK].rearrange("(h p) n -> p h n", p=P)),
                (w_dt[2 * NS:, :], a["L0_attn_dt_proj_w"]),
                (conv_w[:, :, :], a["L0_attn_conv_w"].rearrange("(h p) k -> p h k", p=P)),
                (conv_b[:, :], a["L0_attn_conv_b"].rearrange("(h p) -> p h", p=P)),
                (dt_b[:, :], a["L0_attn_dt_proj_b"].rearrange("(h p) -> p h", p=P)),
            ]
            for dst, src in loads:
                w = s.sp(lambda e, d=dst, r=src: e.dma_start(d, r, allow_slow_non_contiguous=True), s_w)
            s.dve(lambda e: e.memset(half[:, :], -0.5))
            for w_ in (front_set, back_set):
                s.dve(lambda e, w_=w_: e.memset(w_.h_t[DH:, 0:1], 0.0))
                s.dve(lambda e, w_=w_: e.memset(w_.k_t[:, :, 0:WIN], 0.0))
                s.dve(lambda e, w_=w_: e.memset(w_.v[:, :, :, :], 1.0))
                s.dve(lambda e, w_=w_: e.memset(w_.vs[0:WIN, 0, :, :], 0.0))
            s.dve(lambda e: e.memset(ff[:, 2, :], 1.0), w)

        def tables(s):
            loads = [
                (cs[:, 0, :], a["c_mask"]),
                (cs[0:96, 1, 0:2 * NS], a["c_sel"]),
                (a_log[:, :, :], a["L0_attn_A_log"].rearrange("(h p) k -> p h k", p=P)),
                (d_par[:, :], a["L0_attn_D_param"].rearrange("(h p) -> p h", p=P)),
                (w_out[:, :, :], a["L0_attn_out_proj_w"].rearrange("(h p) n -> p h n", p=P)),
                (wqkv[:, :, :], a["L0_ffn_wqkv"].rearrange("l p n -> p l n")),
                (w1[:, :, :], a["L0_ffn_w1"].rearrange("l p n -> p l n")),
                (shift[:, :, :], a["c_shift"].rearrange("a p n -> p a n")),
                *((rot[:, q, :, :], a["c_rot"][q, :, :].rearrange("(t p) d -> p t d", p=P)) for q in range(4)),
                *((dst[:, :], a[name].rearrange("l p -> p l"))
                  for dst, name in ((ln_g, "L0_ffn_ln_g"), (ln_b, "L0_ffn_ln_b"))),
            ]
            for l in range(DEPTH):
                loads.append((wo[:, l, :, :], a["L0_ffn_wo"][l, :, :].rearrange("(c p) n -> p c n", p=P)))
                for c, (c0, n) in enumerate(HCH):
                    loads.append((w2[0:n, l, c, :], a["L0_ffn_w2"][l, c0:c0 + n, :]))
                    for g in range(2):
                        src = a["L0_ffn_b1"][l:l + 1, g * HID + c0:g * HID + c0 + n]
                        loads.append((b1[0:n, l, 3 * g + c:3 * g + c + 1], src.rearrange("a p -> p a")))
                loads.append((w2[n:n + 1, l, 2, :], a["L0_ffn_b2"][l:l + 1, :]))
                for q, name in ((0, "L0_ffn_q_scale"), (2, "L0_ffn_k_scale")):
                    src = a[name][l:l + 1, :]
                    hd = DH // 2
                    for dst, piece in ((scl[:, l, q, :], src), (scl[:, l, q + 1, 0:hd], src[:, hd:DH]),
                                       (scl[:, l, q + 1, hd:DH], src[:, 0:hd])):
                        loads.append((dst, piece.to_broadcast([P, piece.shape[1]])))
            for n, (dst, src) in enumerate(loads):
                w = s.sp(lambda e, d=dst, r=src: e.dma_start(d, r, allow_slow_non_contiguous=True), s_w2,
                         cost=0.6 * n)
            s.dve(lambda e: e.tensor_copy(identb[:, :], ident[:, :]), w)
            s.dve(lambda e: e.tensor_copy(maskb[:, :], cs[:, 0, :]), w)
            s.dve(lambda e: e.tensor_copy(selb[:, :], cs[0:96, 1, 0:2 * NS]), w)
            for l in range(DEPTH):
                for q in range(4):
                    s.dve(lambda e, l=l, q=q: e.tensor_tensor(
                        tab[:, l, q, :, :], rot[:, q, :, :], bcast(scl[:, l, q:q + 1, :], [P, NT, DH]), ALU.mult), w)
            ex = s.act(lambda e: e.activation(a_neg[:, :, :], a_log[:, :, :], ACT.Exp), w,
                       table=EXP_LN)
            return s.dve(lambda e: e.tensor_scalar(a_neg[:, :, :], a_neg[:, :, :], -1.0, None, ALU.mult), ex)

        class Stats:
            stat, mv, ve, rs = e_stat, e_mv, e_ve, e_rs

        def norm_scale(s, w, src, *after):
            for t in range(NT):
                n = s.dve(lambda e, t=t: e.bn_stats(w.stat[:, t, :], src(t)), *after, cost=0.2)
            for t in range(NT):
                n2 = s.dve(lambda e, t=t: e.bn_aggr(w.mv[:, t, :], w.stat[:, t, :]), n, cost=0.08)
            n3 = s.dve(lambda e: e.tensor_scalar(w.ve[:, :], w.mv[:, :, 1], EPS, None, ALU.add), n2, cost=0.07)
            return s.pool(lambda e: e.tensor_tensor(w.rs[:, :], w.ve[:, :], half[:, :], ALU.pow), n3, cost=0.96)

        def normalise(s, w, dst, src, *after):
            for t in range(NT):
                n = s.dve(lambda e, t=t: e.tensor_scalar(dst(t), src(t), w.mv[:, t, 0:1], w.rs[:, t:t + 1],
                                                         ALU.subtract, ALU.mult), *after, cost=0.26)
            return n

        def tm(bank):
            return bank.t[:, :].rearrange("p (t d) -> p t d", t=NT)

        def transposes(s, bank, src, *after):
            for n in range(4):
                last = s.pe(lambda e, n=n: e.transpose(bank.t[:, n * P:(n + 1) * P], src(n), ident[:, :]),
                            *after, *bank.readers, cost=0.11)
            return last

        def enter(s, b, scans_done, x1_done, attention_done):
            w = Stats
            B0, B1 = lb[2], lb[3]
            ld = s.sp(lambda e: e.dma_start(x_in[:, :, :], a["L0_attn_x"][bass.ds(b, 1), :, :].rearrange(
                "b (t p) d -> p (b t) d", p=P)), s_x, x1_done)
            rs = norm_scale(s, w, lambda t: x_in[:, t, :], ld)
            zero = s.dve(lambda e: e.memset(x_pad[:, :, 0:NCONV - 1], 0.0), attention_done, cost=0.07)
            xn = normalise(s, w, lambda t: e_xn[:, t, :], lambda t: x_in[:, t, :], rs)
            tr = transposes(s, B0, lambda n: e_xn[:, n, :], xn)
            xt = s.act(lambda e: e.activation(xn_t, B0.t[:, :], ACT.Copy), tr)
            B0.readers = [xt]

            def in_proj(c, bank):
                return s.pe(lambda e: e.matmul(bank.t[:, :], w_in[:, c * P:(c + 1) * P], xn_t, start=True, stop=True),
                            xt, *bank.readers)

            cv_done = []
            for h, bank in enumerate((B1, B0)):
                pj = in_proj(h, bank)
                cp = s.act(lambda e, h=h, bank=bank: e.activation(x_pad[:, h, NCONV - 1:], bank.t[:, :], ACT.Copy), pj)
                n = s.act(lambda e, h=h, bank=bank: e.activation(
                    cv[:, h, :], bank.t[:, :], ACT.Identity, bias=conv_b[:, h:h + 1],
                    scale=conv_w[:, h, NCONV - 1:NCONV]), pj, cost=0.66)
                bank.readers = [n]
                for k in range(NCONV - 1):
                    n = s.dve(lambda e, h=h, k=k: e.scalar_tensor_tensor(
                        cv[:, h, :], x_pad[:, h, k:k + T], conv_w[:, h, k:k + 1], cv[:, h, :],
                        ALU.mult, ALU.add), n, zero, cost=0.66)
                cv_done.append(n)
            for h, bank in enumerate((B1, B0)):
                pj = in_proj(2 + h, bank)
                bank.readers = [s.act(lambda e, h=h, bank=bank: e.activation(zs[:, h, :], bank.t[:, :], ACT.Silu),
                                      pj, x1_done, table=SILU)]
            for h in range(NH2):
                us = s.act(lambda e, h=h: e.activation(u[:, h, :], cv[:, h, :], ACT.Silu), cv_done[h], x1_done,
                           table=SILU)
            for h in range(NH2):
                xp = s.pe(lambda e, h=h: e.matmul(B1.t[0:2 * NS + RANK, :], w_x[:, h, :], u[:, h, :],
                                                  start=h == 0, stop=h == 1), us, *B1.readers)
            hi = s.act(lambda e: e.activation(bc3[0:32, :], B1.t[0:32, :], ACT.Copy), xp, scans_done)
            dr = s.act(lambda e: e.activation(dt_r[32:40, :], B1.t[32:40, :], ACT.Copy), xp)
            r1 = s.dve(lambda e: e.tensor_tensor(bc_r1, B1.t[0:32, :], bc3[0:32, :], ALU.subtract),
                       hi, dr)
            B1.readers = [r1]
            mid = s.dve(lambda e: e.tensor_copy(bc_mid, bc_r1), r1, cost=0.34)
            s.act(lambda e: e.activation(bc3[32:64, :], bc_r1, ACT.Copy), r1)
            s.dve(lambda e: e.tensor_tensor(bc3[64:96, :], bc_r1, bc_mid, ALU.subtract), mid)
            dts = []
            for h, bank in enumerate((B0, B1)):
                dp = s.pe(lambda e, h=h, bank=bank: e.matmul(
                    bank.t[:, :], w_dt[32:40, h * P:(h + 1) * P], dt_r[32:40, :], start=True, stop=True),
                    dr, *bank.readers)
                ab = s.act(lambda e, h=h, bank=bank: e.activation(
                    dt_abs[:, h, :], bank.t[:, :], ACT.Abs, bias=dt_b[:, h:h + 1]), dp, cost=0.57)
                rl = s.dve(lambda e, h=h, bank=bank: e.tensor_scalar(
                    dt[:, h, :], bank.t[:, :], dt_b[:, h:h + 1], 0.0, ALU.add, ALU.max), ab, scans_done, cost=0.66)
                bank.readers = [rl]
                dts.append((ab, rl))
            exs = [s.act(lambda e, h=h: e.activation(dt_abs[:, h, :], dt_abs[:, h, :], ACT.Exp, scale=-1.0),
                         dts[h][0], table=EXP_LN) for h in range(NH2)]
            lns = [s.act(lambda e, h=h: e.activation(dt_abs[:, h, :], dt_abs[:, h, :], ACT.Ln, bias=1.0), exs[h],
                         table=EXP_LN) for h in range(NH2)]
            for h in range(NH2):
                dd = s.pool(lambda e, h=h: e.tensor_tensor(dt[:, h, :], dt[:, h, :], dt_abs[:, h, :], ALU.add),
                            lns[h], dts[h][1])
                done = s.pool(lambda e, h=h: e.tensor_tensor(du[:, h, :], dt[:, h, :], u[:, h, :], ALU.mult), dd, us)
            return done

        def mamba(s, ready, x1_free):
            w = front_set
            B0, B1, B2, B3 = mb
            acc = (B0, B1)
            das, scans, gs, ys = {}, {}, {}, {}

            def sum_state(n):
                for h in range(NH2):
                    ys[n, h] = s.pe(lambda e, h=h: e.matmul(
                        acc[h].t[:, :], ident[:, :], gy[:, n % 2, h, :], start=n == 0, stop=n == NS - 1),
                        gs[n, h], *(acc[h].readers if n == 0 else []), cost=0.85)

            cscp = {}
            for n in range(NS):
                j = n % 2
                at_start = ready if n == 0 else ()
                bb = s.pe(lambda e, n=n: e.matmul(B2.t[:, :], bcast(selb[:, n:n + 1], [96, P]), bc3[:, :],
                                                  start=True, stop=True),
                          *at_start, *B2.readers, cost=0.22)
                cc = s.pe(lambda e, n=n: e.matmul(B3.t[:, :], bcast(selb[:, NS + n:NS + n + 1], [96, P]), bc3[:, :],
                                                  start=True, stop=True),
                          *B3.readers, cost=0.22)
                for h in range(NH2):
                    das[n, h] = s.act(lambda e, n=n, h=h, j=j: e.activation(
                        da[:, j, h, :], dt[:, h, :], ACT.Exp, scale=a_neg[:, h, n:n + 1]),
                        scans.get((n - 2, h)), *at_start, cost=0.61, table=EXP_LN)
                cscp[n] = s.act(lambda e, j=j: e.activation(cs[:, j, :], B3.t[:, :], ACT.Copy),
                                cc, gs.get((n - 2, 1)))
                B3.readers = [cscp[n]]
                for h in range(NH2):
                    db = s.dve(lambda e, h=h: e.tensor_tensor(dbu[:, h, :], du[:, h, :], B2.t[:, :], ALU.mult),
                               bb, *at_start)
                    scans[n, h] = s.dve(lambda e, h=h, j=j: e.tensor_tensor_scan(
                        hs[:, j, h, :], da[:, j, h, :], dbu[:, h, :], 0.0, ALU.mult, ALU.add),
                        db, das[n, h], gs.get((n - 2, h)))
                B2.readers = [db]
                for h in range(NH2):
                    gs[n, h] = s.pool(lambda e, h=h, j=j: e.tensor_tensor(
                        gy[:, j, h, :], hs[:, j, h, :], cs[:, j, :], ALU.mult),
                        scans[n, h], cscp[n], ys.get((n - 2, h)), cost=1.2)
                if n:
                    sum_state(n - 1)
            sum_state(NS - 1)
            scans_done = ys[NS - 1, 1]
            for h in range(NH2):
                yd = s.dve(lambda e, h=h: e.scalar_tensor_tensor(
                    yg[:, h, :], u[:, h, :], d_par[:, h:h + 1], acc[h].t[:, :], ALU.mult, ALU.add), ys[NS - 1, h])
                acc[h].readers = [yd]
                yz = s.pool(lambda e, h=h: e.tensor_tensor(yg[:, h, :], yg[:, h, :], zs[:, h, :], ALU.mult), yd)
            for t in range(NT):
                for h in range(NH2):
                    op = s.pe(lambda e, t=t, h=h: e.matmul(
                        B2.t[:, t * P:(t + 1) * P], yg[:, h, t * P:(t + 1) * P], w_out[:, h, :],
                        start=h == 0, stop=h == 1), yz, *B2.readers, cost=0.21)
            rs = norm_scale(s, w, lambda t: B2.t[:, t * P:(t + 1) * P], op)
            xn = normalise(s, w, lambda t: m_ln[:, t, :], lambda t: B2.t[:, t * P:(t + 1) * P], rs)
            B2.readers = [xn]
            x1 = s.pool(lambda e: e.tensor_tensor(x1_next[:, :, :], m_ln[:, :, :], x_in[:, :, :], ALU.add),
                        xn, x1_free)
            return scans_done, x1

        def front(s, ready, x1_free, x2_free):
            scans_done, x1 = mamba(s, ready, x1_free)
            w = front_set
            rs = norm_scale(s, w, lambda t: x1_next[:, t, :], x1)
            xn = normalise(s, w, lambda t: x2_next[:, t, :], lambda t: x1_next[:, t, :], rs, x2_free)
            return scans_done, x1, attention(s, w, 0, x2_next, xn)

        def back(s, b, ready, stored, entered):
            w = back_set
            c2 = s.dve(lambda e: e.tensor_copy(xa[:, :, :], x2_next[:, :, :]), *ready, cost=0.34)
            c1 = s.act(lambda e: e.activation(x_cur[:, :, :], x1_next[:, :, :], ACT.Copy), *ready, cost=0.52)
            x = feed_forward(s, w, 0, c2, lb[0:2] * 2, stored)
            x2 = attention(s, w, 1, xa, x, entered)
            x = feed_forward(s, w, 1, x2, lb[0:2] * 2)
            rs = norm_scale(s, w, lambda t: xa[:, t, :], x)
            xn = normalise(s, w, lambda t: xa[:, t, :], lambda t: xa[:, t, :], rs)
            wr = s.dve(lambda e: e.tensor_tensor(o_buf[:, :, :], xa[:, :, :], x_cur[:, :, :], ALU.add), xn)
            store = s.sp(lambda e: e.dma_start(out[bass.ds(b, 1), :, :].rearrange(
                "b (t p) d -> p (b t) d", p=P), o_buf[:, :, :]), s_out, wr)
            return c1, c2, x2, wr, store

        def attention(s, w, l, x, x_done, buffers_free=None):
            L0, L1, L2, L3 = w.banks
            h_t, sq, m1, m2, qr, kr, q_t, k_t, v, vs = (w.h_t, w.sq, w.m1, w.m2, w.qr, w.kr, w.q_t, w.k_t, w.v, w.vs)
            ss, rn, rn_t, rq8, mx, nb, rd, pr, p_t, o, o_t = (w.ss, w.rn, w.rn_t, w.rq8, w.mx, w.nb, w.rd, w.pr,
                                                              w.p_t, w.o, w.o_t)
            tr = transposes(s, L0, lambda n: x[:, n, :], x_done)
            c0 = s.act(lambda e: e.activation(h_t[0:DH, :], L0.t[0:DH, :], ACT.Copy), tr)
            c1 = s.act(lambda e: e.activation(h_t[DH:, 1:T], L0.t[DH:, 0:T - 1], ACT.Copy), tr)
            L0.readers = [c1]
            sq_read, m_read, added = {}, {}, {}
            heads = lambda x: x.rearrange("p (h d) -> p h d", h=HEADS)
            halves = lambda x: x.rearrange("p (h a d) -> p h a d", h=HEADS, a=2)

            ring = cycle((L1, L2, L3))

            def project(t, part):
                bank = L0 if part == 2 else next(ring)
                mm = s.pe(lambda e: e.matmul(
                    bank.t[:, :], h_t[:, t * P:(t + 1) * P], wqkv[:, l, part * INNER:(part + 1) * INNER],
                    start=True, stop=True), c0, c1, *bank.readers)
                return bank, mm

            def rotate(t, part, chain=()):
                bank, mm = project(t, part)
                sqd = s.act(lambda e: e.activation(sq[:, t % 2, :], bank.t[:, :], ACT.Square), mm, sq_read.get(t % 2),
                            buffers_free)
                sq_read[t % 2] = s.dve(lambda e: e.tensor_reduce(
                    ss[:, part, t, :], heads(sq[:, t % 2, :]), AX, ALU.add), sqd)
                some(chain, 2)
                table = [bcast(tab[:, l, 2 * part + n, t:t + 1, :], [P, HEADS, DH]).rearrange(
                    "p h (a d) -> p h a d", a=2) for n in range(2)]
                s.dve(lambda e: e.tensor_tensor(halves(m1[:, t % 2, :]), halves(bank.t[:, :]), table[0], ALU.mult),
                      sqd, m_read.get(t % 2))
                some(chain, 2)
                mc = s.dve(lambda e: e.tensor_tensor(halves(m2[:, t % 2, :]), halves(bank.t[:, :])[:, :, ::-1, :],
                                                     table[1], ALU.mult), sqd)
                some(chain, 2)
                bank.readers = [mc]
                adder = s.dve if (part, t) == (0, NT - 1) else s.pool
                m_read[t % 2] = added[part, t] = adder(lambda e: e.tensor_tensor(
                    (qr, kr)[part][:, t, :], m1[:, t % 2, :], m2[:, t % 2, :], ALU.add), mc)

            def some(chain, n):
                for _ in zip(range(n), chain):
                    pass

            def value(t):
                bank, mm = project(t, 2)
                vc = s.act(lambda e: e.activation(v[:, t, :, 0:DH], heads(bank.t[:, :]), ACT.Copy), mm)
                bank.readers = [vc]
                return vc

            def inverse_norms(part):
                flat = lambda x: x[:, part, :, :].rearrange("p t h -> p (t h)")
                r = flat(rn)
                n = s.dve(lambda e: e.tensor_scalar(flat(ss), flat(ss), 1e-24, None, ALU.max), *sq_read.values(),
                          cost=0.1)
                yield n
                n = s.dve(lambda e: e.tensor_single_scalar(flat(rn_t).bitcast(I32), flat(ss).bitcast(I32), 1,
                                                           ALU.arith_shift_right), n, cost=0.1)
                yield n
                n = s.dve(lambda e: e.tensor_scalar(r.bitcast(I32), flat(rn_t).bitcast(I32), -1.0,
                                                    float(MAGIC), ALU.mult, ALU.add), n, cost=0.1)
                yield n
                for _ in range(3):
                    n = s.dve(lambda e: e.scalar_tensor_tensor(flat(rn_t), flat(ss), -0.5, r,
                                                               ALU.mult, ALU.mult), n, cost=0.1)
                    yield n
                    n = s.dve(lambda e: e.tensor_tensor(flat(rn_t), flat(rn_t), r, ALU.mult), n, cost=0.1)
                    yield n
                    n = s.dve(lambda e: e.scalar_tensor_tensor(r, flat(rn_t), 1.5, r, ALU.add, ALU.mult), n,
                              cost=0.1)
                    yield n
                if part == 0:
                    n = s.dve(lambda e: e.tensor_scalar(rq8[:, :, :], rn[:, 0, :, :], 8.0, None, ALU.mult), n,
                              cost=0.1)
                    yield n
                norms_done[part] = n

            def channel_major(t, bank, dst, off, src, *after):
                tr = transposes(s, bank, lambda c: src[:, t, c * P:(c + 1) * P], *after)
                cp = s.act(lambda e: e.activation(dst[:, :, off + t * P:off + (t + 1) * P], bank.t[:, :].rearrange(
                    "p (c n) -> p c n", c=NC), ACT.Copy), tr)
                bank.readers = [cp]
                return cp

            def query(t, bank):
                return channel_major(t, bank, q_t, 0, qr, added[0, t])

            def keys(t, bank):
                return channel_major(t, bank, k_t, WIN, kr, kns[t])

            def normalise_key(t):
                kns[t] = s.pool(lambda e: e.tensor_tensor(
                    heads(kr[:, t, :]), heads(kr[:, t, :]), bcast(rn[:, 1, t, :].unsqueeze(2), [P, HEADS, DH]),
                    ALU.mult), norms_done[1], added[1, t])

            norms_done, kns = {}, {}
            k_chain, q_chain = inverse_norms(1), inverse_norms(0)
            rotate(0, 1)
            rotate(1, 1)
            value(0)
            rotate(2, 1)
            rotate(3, 1)
            value(1)
            rotate(0, 0, k_chain)
            value(2)
            rotate(1, 0, k_chain)
            some(k_chain, 99)
            normalise_key(0)
            vc = value(3)
            rotate(2, 0)
            normalise_key(1)
            query(0, L0)
            keys(0, L0)
            rotate(3, 0)
            some(q_chain, 99)
            q8 = norms_done[0]
            normalise_key(2)
            query(1, L0)
            normalise_key(3)
            keys(1, L0)
            query(2, L1)
            keys(2, L2)
            query(3, L0)
            qk = keys(3, L3)
            v1 = s.sp(lambda e: e.dma_start(vs[0:WIN, 1:NT, :, :], v[WIN:, 0:NT - 1, :, :]), s_vs[2 * l], vc)
            v2 = s.sp(lambda e: e.dma_start(vs[WIN:, :, :, :], v[0:WIN, :, :, :]), s_vs[2 * l + 1], vc)
            weights, pts, copies, avs = {}, {}, {}, {}
            ot = L3.t[:, 0:NT * (DH + 1)].rearrange("p (t d) -> p t d", t=NT)

            def scores(hd):
                c, r, bank = hd // 2, DH * (hd % 2), (L0, L1)[hd % 2]
                s.pe(lambda e: e.matmul(bank.t[:, :], identb[:, :], maskb[:, :], start=True, stop=False,
                                        skip_group_check=True), *bank.readers, cost=0.22)
                for p in range(NT):
                    for j in range(2):
                        last = s.pe(lambda e, p=p, j=j: e.matmul(
                            bank.t[WIN * j:WIN * j + WIN, p * P:(p + 1) * P],
                            q_t[r:r + DH, c, p * P + WIN * j:p * P + WIN * j + WIN],
                            k_t[r:r + DH, c, p * P + WIN * j:p * P + WIN * j + P],
                            start=False, stop=True, skip_group_check=True), qk, cost=0.12)
                return last

            def softmax(hd, sc):
                bank = (L0, L1)[hd % 2]
                m = s.dve(lambda e: e.tensor_reduce(
                    mx[:, hd, :], bank.t[:, :].rearrange("p (t k) -> p t k", t=NT), AX, ALU.max), sc)
                n = s.dve(lambda e: e.scalar_tensor_tensor(
                    nb[:, hd, :], mx[:, hd, :], -1.0, rq8[:, :, hd], ALU.mult, ALU.mult), m, q8, cost=0.08)
                for p in range(NT):
                    last = s.act(lambda e, p=p: e.activation(
                        pr[:, hd % 2, p, :], bank.t[:, p * P:(p + 1) * P], ACT.Exp, bias=nb[:, hd, p:p + 1],
                        scale=rq8[:, p, hd:hd + 1]), n, pts.get(hd - 2), cost=0.35, table=EXP_LN)
                bank.readers = [last]
                return last

            def keys_in_partitions(hd):
                pts[hd] = transposes(s, L2, lambda n: pr[:, hd % 2, n, :], weights[hd])
                if hd % 4 != 3:
                    cp = s.dve(lambda e: e.tensor_copy(p_t[:, hd % 2, :], L2.t[:, :]), pts[hd], avs.get(hd - 2))
                else:
                    cp = s.act(lambda e: e.activation(p_t[:, hd % 2, :], L2.t[:, :], ACT.Copy), pts[hd],
                               avs.get(hd - 2))
                L2.readers = [cp]
                return cp

            def values(hd):
                for p in range(NT):
                    for j in range(2):
                        avs[hd] = s.pe(lambda e, p=p, j=j: e.matmul(
                            ot[WIN * j:WIN * j + WIN, p, :],
                            p_t[:, hd % 2, p * P + WIN * j:p * P + WIN * j + WIN],
                            (vs, v)[j][:, p, hd, :], start=True, stop=True),
                            copies[hd], v1, v2, *L3.readers, cost=0.065)
                rc = s.dve(lambda e: e.reciprocal(rd[:, hd, :], ot[:, :, DH]), avs[hd], cost=0.09)
                od = s.dve(lambda e: e.tensor_tensor(
                    o[:, :, hd * DH:(hd + 1) * DH], ot[:, :, 0:DH],
                    bcast(rd[:, hd, :].unsqueeze(2), [P, NT, DH]), ALU.mult), rc, cost=0.33)
                L3.readers = [od]
                return od

            for i in range(HEADS + 2):
                if i < HEADS:
                    weights[i] = softmax(i, scores(i))
                if 0 < i <= HEADS:
                    copies[i - 1] = keys_in_partitions(i - 1)
                if i > 1:
                    od = values(i - 2)
            oc = {}
            for c in range(NC):
                bank = (L0, L1, L2, L0)[c]
                tr = transposes(s, bank, lambda n, c=c: o[:, n, c * P:(c + 1) * P], od)
                oc[c] = s.act(lambda e, c=c, bank=bank: e.activation(o_t[:, c, :], bank.t[:, :], ACT.Copy), tr)
                bank.readers = [oc[c]]
            for t in range(NT):
                for c in range(NC):
                    mm = s.pe(lambda e, t=t, c=c: e.matmul(
                        L3.t[:, t * P:(t + 1) * P], o_t[:, c, t * P:(t + 1) * P], wo[:, l, c, :],
                        start=c == 0, stop=c == NC - 1), oc[c], *L3.readers, cost=0.21)
            x2 = s.dve(lambda e: e.tensor_tensor(x[:, :, :], x[:, :, :], tm(L3), ALU.add), mm)
            L3.readers = [x2]
            return x2

        def feed_forward(s, w, l, x2, banks, h2_free=None):
            L0, L1, L2, L3 = banks
            sh = L0.t[:, 0:NT * DH].rearrange("p (t d) -> p t d", t=NT)
            s.pe(lambda e: e.matmul(sh, shift[:, 0, :], xa[:, :, DH:], start=True, stop=False,
                                    skip_group_check=True), x2, *L0.readers, cost=0.43)
            mm = s.pe(lambda e: e.matmul(sh[:, 1:, :], shift[:, 1, :], xa[:, 0:NT - 1, DH:], start=False, stop=True,
                                         skip_group_check=True), cost=0.32)
            ha = s.dve(lambda e: e.tensor_copy(h2[:, :, 0:DH], xa[:, :, 0:DH]), x2, h2_free, cost=0.18)
            hb = s.act(lambda e: e.activation(h2[:, :, DH:], sh, ACT.Copy), mm, h2_free, cost=0.35)
            L0.readers = [hb]
            rs = norm_scale(s, w, lambda t: h2[:, t, :], ha, hb)
            hn = normalise(s, w, lambda t: h2[:, t, :], lambda t: h2[:, t, :], rs)
            tr = transposes(s, L1, lambda n: h2[:, n, :], hn)
            ht = s.act(lambda e: e.activation(h2_t, L1.t[:, :], ACT.Identity, bias=ln_b[:, l:l + 1],
                                              scale=ln_g[:, l:l + 1]), tr)
            L1.readers = [ht]
            ge_read = {}
            for c, (c0_, n) in enumerate(HCH):
                ab, gb = ((L2, L3), (L0, L1), (L2, L3))[c]
                mg = s.pe(lambda e, c0_=c0_, n=n, gb=gb: e.matmul(
                    gb.t[0:n, :], w1[:, l, HID + c0_:HID + c0_ + n], h2_t, start=True, stop=True),
                    ht, *gb.readers, cost=0.85)
                ma = s.pe(lambda e, c0_=c0_, n=n, ab=ab: e.matmul(
                    ab.t[0:n, :], w1[:, l, c0_:c0_ + n], h2_t, start=True, stop=True),
                    ht, *ab.readers, cost=0.85)
                gd = s.act(lambda e, c=c, n=n, gb=gb: e.activation(
                    ge[0:n, c % 2, :], gb.t[0:n, :], ACT.Gelu, bias=b1[0:n, l, 3 + c:4 + c]), mg,
                    ge_read.get(c % 2), cost=0.57, table=GELU)
                gb.readers = [gd]
                ge_read[c % 2] = fd = s.dve(lambda e, c=c, n=n, ab=ab: e.scalar_tensor_tensor(
                    ff[0:n, c, :], ab.t[0:n, :], b1[0:n, l, c:c + 1], ge[0:n, c % 2, :], ALU.add, ALU.mult), ma, gd)
                ab.readers = [fd]
            for t in range(NT):
                for c, (c0_, n) in enumerate(HCH):
                    k = n + (c == 2)
                    mm = s.pe(lambda e, t=t, c=c, k=k: e.matmul(
                        L0.t[:, t * P:(t + 1) * P], ff[0:k, c, t * P:(t + 1) * P], w2[0:k, l, c, :],
                        start=c == 0, stop=c == 2), fd, *L0.readers, cost=0.21)
            x3 = s.dve(lambda e: e.tensor_tensor(xa[:, :, :], xa[:, :, :], tm(L0), ALU.add), mm)
            L0.readers = [x3]
            return x3

        s = Stage(t_sems)
        load(s)
        run_block(nc, s.ops, block_sems)

        def rounds(*steps, first=False):
            sb_, sf, se, st = Stage(b_sems), Stage(f_sems), Stage(e_sems), Stage(t_sems)
            for k in mb + lb:
                k.readers = []
            entered = fronted = backed = stored = attention_done = None
            if first:
                fronted = tables(st)
            x1_copied = x2_copied = scans_done = x1 = None
            for b_back, b_front, b_enter in steps:
                if b_back is not None:
                    x1_copied, x2_copied, attention_done, backed, stored = back(
                        sb_, b_back, (fronted, backed), stored, entered)
                if b_front:
                    scans_done, x1, fronted = front(sf, (entered, fronted), x1_copied, x2_copied)
                if b_enter is not None:
                    entered = enter(se, b_enter, scans_done, x1, attention_done)
            sb_.add("sp", lambda e: None, stored)
            run_block(nc, merged([sb_, sf, se, st]), block_sems)

        rounds((None, False, 0), (None, True, 1), first=True)
        with nc.Fori(0, (B - 2) // 2) as i:
            rounds((2 * i, True, 2 * i + 2), (2 * i + 1, True, 2 * i + 3))
        rounds((B - 2, True, None), (B - 1, False, None))


_INS = ["L0_attn_x", "L0_attn_in_proj_w", "L0_attn_conv_w", "L0_attn_conv_b", "L0_attn_x_proj_w",
        "L0_attn_dt_proj_w", "L0_attn_dt_proj_b", "L0_attn_A_log", "L0_attn_D_param", "L0_attn_out_proj_w",
        "L0_ffn_wqkv", "L0_ffn_q_scale", "L0_ffn_k_scale", "L0_ffn_wo", "L0_ffn_ln_g", "L0_ffn_ln_b",
        "L0_ffn_w1", "L0_ffn_b1", "L0_ffn_w2", "L0_ffn_b2"]


def constants():
    f = np.float32
    c = {"c_ident": np.eye(P, dtype=f)}
    sh = np.zeros((2, P, P), f)
    sh[0, np.arange(P - 1), np.arange(1, P)] = 1
    sh[1, P - 1, 0] = 1
    c["c_shift"] = sh
    c["c_sel"] = np.tile(np.eye(2 * NS, dtype=f), (3, 1))
    q, k = np.arange(P)[:, None], np.arange(P)[None, :]
    i = q % WIN
    bad = (i + WIN < k) | (i + WIN > k + WIN)
    m = np.zeros((P, NT, P), bool)
    m[:] = bad[:, None, :]
    m[0:WIN, 0, 0:WIN] = True
    c["c_mask"] = np.where(m, f(NEG), f(0)).reshape(P, NT * P)
    hi = np.arange(0, DH, 2, dtype=f)
    inv = f(1) / f(10000.0) ** (hi / f(DH))
    t = np.arange(T, dtype=f)
    fr = np.concatenate([t[:, None] * inv[None, :]] * 2, -1)
    base = (hi + f(0.4 * DH)) / f(1.4 * DH)
    power = (t - T // 2) / f(WIN // 2)
    sc = np.concatenate([base[None, :] ** power[:, None]] * 2, -1)
    sign = np.where(np.arange(DH) < DH // 2, f(-1), f(1))
    cos, sin = np.cos(fr), np.sin(fr) * sign
    c["c_rot"] = np.stack([cos * sc, sin * sc, cos / sc, sin / sc]).astype(f)
    return c


def kernel(**inputs):
    import concourse.bacc as _bacc
    from concourse.bass_utils import run_bass_kernel_spmd as _run

    nc = _bacc.Bacc("TRN2", target_bir_lowering=False, num_devices=1)
    arrays, aps = {}, {}
    for name, x in [*((n, inputs[n]) for n in _INS), *constants().items()]:
        x = np.ascontiguousarray(x)
        arrays[f"in_{name}"] = x
        aps[name] = nc.dram_tensor(f"in_{name}", x.shape, mybir.dt.from_np(x.dtype), kind="ExternalInput").ap()
    out = nc.dram_tensor("out_dram", (B, T, D), F32, kind="ExternalOutput").ap()
    build(nc, aps, out)
    r = _run(nc, [arrays], core_ids=[0])
    return r.results[0]["out_dram"]
```
